# Optimizing a Trainium2 kernel written in Bass

```python
import numpy as np
import jax
import jax.numpy as jnp

def _softmax(x, axis=-1):
    return jax.nn.softmax(x, axis=axis)

def _gelu(x):
    return jax.nn.gelu(x, approximate=True)

def _silu(x):
    return jax.nn.silu(x)

def _sigmoid(x):
    return jax.nn.sigmoid(x)

def _layernorm(x, axis=-1, eps=1e-05):
    m = jnp.mean(x, axis=axis, keepdims=True)
    v = jnp.var(x, axis=axis, keepdims=True)
    return (x - m) / jnp.sqrt(v + eps)

def _scatter_add(tgt, idx, src, axis=0):
    return tgt.at[idx].add(src)

def _segment_sum(src, seg, n):
    return jax.ops.segment_sum(src, seg, n)
kernel_name = 'mk_gnn_ffn_d1_gnn_r32_e46160'

def setup_inputs(seed: int=0):
    np.random.seed(seed)
    _w = jnp.asarray

    def _rec_inputs():
        import jax
        import jax.numpy as jnp
        _gk = jax.random.key(seed)
        x = -8.776e-05 + 1 * jax.random.normal(jax.random.fold_in(_gk, 1), (10000, 1024), jnp.float32)
        src = jax.random.randint(jax.random.fold_in(_gk, 2), (5000,), 0, 10000, jnp.int32)
        dst = jnp.minimum((10000 * jax.random.uniform(jax.random.fold_in(_gk, 3), (5000,)) ** 2.0).astype(jnp.int32), 9999)
        _o = jnp.argsort(dst, stable=True)
        src = src[_o]
        dst = dst[_o]
        return (x, src, dst)
    x, src, dst = _rec_inputs()

    def _L0_gnn_setup():
        import math
        import jax, jax.numpy as jnp
        import numpy as np
        N_NODES = 5000
        N_EDGES = 5000
        D_IN = 1024
        D_OUT = 1024
        BN_EPS = 1e-05

        def _positional_encoding(n, d):
            pos = jnp.arange(n, dtype=jnp.float32)[:, None]
            div = jnp.exp(jnp.arange(0, d, 2, dtype=jnp.float32) * (-math.log(10000.0) / d))
            ang = pos * div
            pe = jnp.stack([jnp.sin(ang), jnp.cos(ang)], axis=-1).reshape(n, d)
            return pe

        def _gcn_conv(x, W, b, src, dst, dinv):
            xw = x @ W
            norm = (dinv[src] * dinv[dst])[:, None]
            agg = jax.ops.segment_sum(xw[src] * norm, dst, num_segments=x.shape[0])
            agg = agg + xw * (dinv * dinv)[:, None]
            return agg + b
        key = jax.random.key(seed)
        ks = jax.random.split(key, 8)
        x = jax.random.normal(ks[0], (N_NODES, D_IN), dtype=jnp.float32)
        src = jax.random.randint(ks[1], (N_EDGES,), 0, N_NODES, dtype=jnp.int32)
        dst = jax.random.randint(ks[2], (N_EDGES,), 0, N_NODES, dtype=jnp.int32)
        s1 = 1.0 / math.sqrt(D_IN)
        s2 = 1.0 / math.sqrt(D_OUT)
        W1 = jax.random.uniform(ks[3], (D_IN, D_OUT), jnp.float32, -s1, s1)
        b1 = jnp.zeros((D_OUT,), jnp.float32)
        gamma = jnp.ones((D_OUT,), jnp.float32)
        beta = jnp.zeros((D_OUT,), jnp.float32)
        W2 = jax.random.uniform(ks[4], (D_OUT, D_OUT), jnp.float32, -s2, s2)
        b2 = jnp.zeros((D_OUT,), jnp.float32)
        return {'x': x, 'src': src, 'dst': dst, 'W1': W1, 'b1': b1, 'gamma': gamma, 'beta': beta, 'W2': W2, 'b2': b2}
    _L0_gnn_all = _L0_gnn_setup()
    _L0_gnn_in = {k: v for k, v in _L0_gnn_all.items() if k in ('W1', 'b1', 'gamma', 'beta', 'W2', 'b2')}
    del _L0_gnn_all

    def _L0_ffn_setup():
        import jax, jax.numpy as jnp
        import numpy as np
        S, B, H, F, E, K = (64, 2, 1024, 64, 8, 2)

        def _moe_forward(hidden_states, router_w, w1, b1, w2, b2):
            s, b, h = hidden_states.shape
            T = s * b
            x = hidden_states.reshape(T, h)
            logits = jnp.einsum('th,eh->te', x, router_w)
            topk_logits, topk_idx = jax.lax.top_k(logits, K)
            probs = jax.nn.softmax(topk_logits, axis=-1)
            combine = jnp.zeros((T, E), dtype=x.dtype)
            combine = combine.at[jnp.arange(T)[:, None], topk_idx].add(probs.astype(x.dtype))
            hmid = jnp.einsum('th,efh->etf', x, w1) + b1[:, None, :]
            hmid = jax.nn.gelu(hmid, approximate=False)
            y = jnp.einsum('etf,ehf->eth', hmid, w2) + b2[:, None, :]
            out = jnp.einsum('eth,te->th', y, combine)
            return out.reshape(s, b, h)
        key = jax.random.key(seed)
        ks = jax.random.split(key, 6)
        std = 0.02
        return {'hidden_states': jax.random.normal(ks[0], (S, B, H), dtype=jnp.float32), 'router_w': jax.random.normal(ks[1], (E, H), dtype=jnp.float32) * std, 'w1': jax.random.normal(ks[2], (E, F, H), dtype=jnp.float32) * (1.0 / np.sqrt(H)), 'b1': jnp.zeros((E, F), dtype=jnp.float32), 'w2': jax.random.normal(ks[3], (E, H, F), dtype=jnp.float32) * (1.0 / np.sqrt(F)), 'b2': jnp.zeros((E, H), dtype=jnp.float32)}
    _L0_ffn_all = _L0_ffn_setup()
    _L0_ffn_in = {k: v for k, v in _L0_ffn_all.items() if k in ('router_w', 'w1', 'b1', 'w2', 'b2')}
    del _L0_ffn_all
    return {'x': x, 'src': src, 'dst': dst, 'L0_gnn_W1': _L0_gnn_in['W1'], 'L0_gnn_b1': _L0_gnn_in['b1'], 'L0_gnn_gamma': _L0_gnn_in['gamma'], 'L0_gnn_beta': _L0_gnn_in['beta'], 'L0_gnn_W2': _L0_gnn_in['W2'], 'L0_gnn_b2': _L0_gnn_in['b2'], 'L0_ffn_router_w': _L0_ffn_in['router_w'], 'L0_ffn_w1': _L0_ffn_in['w1'], 'L0_ffn_b1': _L0_ffn_in['b1'], 'L0_ffn_w2': _L0_ffn_in['w2'], 'L0_ffn_b2': _L0_ffn_in['b2']}

def reference(x, src, dst, L0_gnn_W1, L0_gnn_b1, L0_gnn_gamma, L0_gnn_beta, L0_gnn_W2, L0_gnn_b2, L0_ffn_router_w, L0_ffn_w1, L0_ffn_b1, L0_ffn_w2, L0_ffn_b2):
    import jax
    import jax.numpy as jnp

    def _L0_gnn_ref(x, src, dst, W1, b1, gamma, beta, W2, b2):
        import math
        import jax, jax.numpy as jnp
        import numpy as np
        N_NODES = 5000
        N_EDGES = 5000
        D_IN = 1024
        D_OUT = 1024
        BN_EPS = 1e-05

        def _positional_encoding(n, d):
            pos = jnp.arange(n, dtype=jnp.float32)[:, None]
            div = jnp.exp(jnp.arange(0, d, 2, dtype=jnp.float32) * (-math.log(10000.0) / d))
            ang = pos * div
            pe = jnp.stack([jnp.sin(ang), jnp.cos(ang)], axis=-1).reshape(n, d)
            return pe

        def _gcn_conv(x, W, b, src, dst, dinv):
            xw = x @ W
            norm = (dinv[src] * dinv[dst])[:, None]
            agg = jax.ops.segment_sum(xw[src] * norm, dst, num_segments=x.shape[0])
            agg = agg + xw * (dinv * dinv)[:, None]
            return agg + b
        n = x.shape[0]
        x = x + _positional_encoding(n, x.shape[1])
        deg = jax.ops.segment_sum(jnp.ones_like(dst, dtype=x.dtype), dst, num_segments=n) + 1.0
        dinv = deg ** (-0.5)
        h = _gcn_conv(x, W1, b1, src, dst, dinv)
        mu = h.mean(axis=0)
        var = h.var(axis=0)
        h = (h - mu) * jax.lax.rsqrt(var + BN_EPS) * gamma + beta
        h = jax.nn.relu(h)
        h = _gcn_conv(h, W2, b2, src, dst, dinv)
        return jax.nn.relu(h)

    def _L0_ffn_ref(hidden_states, router_w, w1, b1, w2, b2):
        import jax, jax.numpy as jnp
        import numpy as np
        S, B, H, F, E, K = (64, 2, 1024, 64, 8, 2)

        def _moe_forward(hidden_states, router_w, w1, b1, w2, b2):
            s, b, h = hidden_states.shape
            T = s * b
            x = hidden_states.reshape(T, h)
            logits = jnp.einsum('th,eh->te', x, router_w)
            topk_logits, topk_idx = jax.lax.top_k(logits, K)
            probs = jax.nn.softmax(topk_logits, axis=-1)
            combine = jnp.zeros((T, E), dtype=x.dtype)
            combine = combine.at[jnp.arange(T)[:, None], topk_idx].add(probs.astype(x.dtype))
            hmid = jnp.einsum('th,efh->etf', x, w1) + b1[:, None, :]
            hmid = jax.nn.gelu(hmid, approximate=False)
            y = jnp.einsum('etf,ehf->eth', hmid, w2) + b2[:, None, :]
            out = jnp.einsum('eth,te->th', y, combine)
            return out.reshape(s, b, h)
        return _moe_forward(hidden_states, router_w, w1, b1, w2, b2)
    x = x + _L0_gnn_ref(_layernorm(x, axis=-1), src, dst, L0_gnn_W1, L0_gnn_b1, L0_gnn_gamma, L0_gnn_beta, L0_gnn_W2, L0_gnn_b2)
    x = x + _L0_ffn_ref(_layernorm(x, axis=-1)[None], L0_ffn_router_w, L0_ffn_w1, L0_ffn_b1, L0_ffn_w2, L0_ffn_b2)[0]
    return x

_drawn_inputs = setup_inputs


def setup_inputs(seed=0):
    import zlib

    import numpy as np

    out = dict(_drawn_inputs(seed))
    spreads = {'L0_gnn_b1': (0.0, 0.1),
     'L0_gnn_gamma': (1.0, 0.2),
     'L0_gnn_beta': (0.0, 0.1),
     'L0_gnn_b2': (0.0, 0.1),
     'L0_ffn_b1': (0.0, 0.1),
     'L0_ffn_b2': (0.0, 0.1)}
    factors = {}
    for name, (base, spread) in spreads.items():
        noise = np.random.default_rng([zlib.crc32(name.encode()), seed]).standard_normal(out[name].shape)
        drawn = base * np.exp(spread * noise) if base else spread * noise
        out[name] = jnp.asarray(drawn.astype(out[name].dtype))
    for name, factor in factors.items():
        out[name] = (out[name] * factor).astype(out[name].dtype)
    return out
```

```python
import concourse.bass as bass
from concourse import mybir
from contextlib import ExitStack

F32 = mybir.dt.float32
F32R = mybir.dt.float32r
BF16 = mybir.dt.bfloat16
I32 = mybir.dt.int32
U32 = mybir.dt.uint32
U16 = mybir.dt.uint16
ACT = mybir.ActivationFunctionType
ALU = mybir.AluOpType
AX = mybir.AxisListType

P = 128
EPS = 1e-5


class Shapes:

    def __init__(self, x, src, w1t):
        self.N, self.D = x.shape
        self.E = src.shape[0]
        self.KD = self.D // P
        self.H = self.D // 2
        self.NT = -(-self.N // P)
        self.LAST = self.N - (self.NT - 1) * P
        self.A = -(-self.NT // 16) * 16
        self.EP = -(-self.E // (4 * P)) * 2
        self.ET = 2 * self.EP
        self.EPAD = self.ET * P
        self.F = w1t.shape[1]
        self.KF = self.F // P
        self.PAD_DST = P * P - 1
        self.SKIP = 1 << 16


def edge_tables(nc, s, io, keep, mk):
    ctx = ExitStack()
    with ctx:
        def sb(name, shape, dt=F32):
            return ctx.enter_context(nc.sbuf_tensor("tb_" + name, shape, dt))

        def sem(name):
            return mk.enter_context(nc.semaphore("tb_" + name))

        ET, EP, A, EPAD = s.ET, s.EP, s.A, s.EPAD
        G = 6
        groups = [(g, min(g + G, ET)) for g in range(0, ET, G)]
        full = s.E // P
        rest = s.E - full * P
        rows_i = sb("rows_i", [ET, 2, P], I32)
        rows_w = sb("rows_w", [ET, 3, P], I32)
        rows_f = sb("rows_f", [ET, 5, P])
        dst_all = sb("dst_all", [P, EPAD], I32)
        src_all = sb("src_all", [P, EPAD], I32)
        low_dst = sb("low_dst", [P, EPAD])
        low_src = sb("low_src", [P, EPAD])
        cols = sb("cols", [P, 5, ET])
        hot_low = sb("hot_low", [P, ET, P], BF16)
        hot_dst = sb("hot_dst", [P, ET, A], BF16)
        hot_src = sb("hot_src", [P, ET, A], BF16)
        iota_p = sb("iota_p", [P, 1])
        iota_a = sb("iota_a", [P, 1, A])
        iota_b = sb("iota_b", [P, 1, P])
        earlier = sb("earlier", [P, 2, 2 * P])
        below = sb("below", [P, P])
        cum = sb("cum", [P, EP + 1, A])
        has = sb("has", [P, A])
        scan = sb("scan", [P, 2, A])
        slot = sb("slot", [P, A])
        std = sb("std", [P, A])
        count = sb("count", [P, ET])
        picked = sb("picked", [P, 3, ET])
        prod = sb("prod", [P, 3, G, A])
        junk = sb("junk", [P, 2 * P])
        zeros = sb("zeros", [P, 1, s.D])
        sel = sb("sel", [P, ET])
        sel2 = sb("sel2", [P, ET])
        ps_hist = [ctx.enter_context(nc.psum_tensor(f"tb_hist{i}", [P, 512], F32)) for i in range(4)]
        ps_pick = [ctx.enter_context(nc.psum_tensor(f"tb_pick{i}", [P, 512], F32)) for i in range(3)]
        ps_misc = ctx.enter_context(nc.psum_tensor("tb_misc", [P, 512], F32))
        pick_banks = [ps_pick, ps_hist[0:3]]

        consts = sem("consts")
        cleared = sem("cleared")
        rows_in = sem("rows_in")
        all_in = sem("all_in")
        zeroed = sem("zeroed")
        rows_ready = sem("rows_ready")
        cols_ps = sem("cols_ps")
        hot_ready = sem("hot_ready")
        hist_ready = sem("hist_ready")
        rowsum_ready = sem("rowsum_ready")
        base_ready = sem("base_ready")
        deg_ready = sem("deg_ready")
        std_ready = sem("std_ready")
        table_ready = sem("table_ready")
        picks_ps = sem("picks_ps")
        picks_read = sem("picks_read")
        step = sem("step")

        with nc.Block() as block:
            @block.gpsimd
            def _(pool):
                pool.memset(zeros[:, :, :], 0.0)
                pool.memset(keep.ident[:, :], 0.0)
                pool.memset(keep.ones[:, :], 1.0)
                pool.memset(keep.zero[:, :], 0.0)
                pool.memset(keep.one[:, :], 1.0)
                pool.memset(below[:, :], 1.0)
                pool.memset(earlier[:, :, :], 1.0).then_inc(consts, 1)
                pool.iota(iota_p[:, :], pattern=[[0, 1]], base=0, channel_multiplier=1,
                          allow_small_or_imprecise_dtypes=True)
                pool.iota(iota_a[:, 0, :], pattern=[[1, A]], base=0, channel_multiplier=0,
                          allow_small_or_imprecise_dtypes=True)
                pool.iota(keep.iota_e[:, :], pattern=[[1, 8]], base=0, channel_multiplier=0,
                          allow_small_or_imprecise_dtypes=True)
                pool.iota(iota_b[:, 0, :], pattern=[[1, P]], base=0, channel_multiplier=0,
                          allow_small_or_imprecise_dtypes=True)
                pool.wait_ge(consts, 1)
                pool.affine_select(out=keep.ident[:, :], in_=keep.ident[:, :], compare_op=ALU.not_equal, fill=1.0,
                                   base=0, pattern=[[-1, P]], channel_multiplier=1)
                pool.affine_select(out=below[:, :], in_=below[:, :], compare_op=ALU.is_gt, fill=0.0,
                                   base=0, pattern=[[1, P]], channel_multiplier=-1)
                pool.affine_select(out=earlier[:, 0, :], in_=earlier[:, 0, :], compare_op=ALU.is_gt, fill=0.0,
                                   base=0, pattern=[[-1, 2 * P]], channel_multiplier=1)
                pool.affine_select(out=earlier[:, 1, :], in_=earlier[:, 1, :], compare_op=ALU.is_gt, fill=0.0,
                                   base=P, pattern=[[-1, 2 * P]], channel_multiplier=1).then_inc(consts, 1)

            @block.sync
            def _(sp):
                sp.wait_ge(cleared, 1)
                for n, v in enumerate((io.src, io.dst)):
                    sp.dma_start(rows_i[0:full, n, :], v[0:full * P].rearrange("(k p) -> k p", p=P)).then_inc(rows_in, 16)
                    sp.dma_start(rows_i[full:full + 1, n, 0:rest],
                                 v[full * P:s.E].rearrange("(k p) -> k p", k=1)).then_inc(rows_in, 16)
                sp.wait_ge(cleared, 2)
                for v, t in ((io.dst, dst_all), (io.src, src_all)):
                    sp.dma_start(t[:, 0:s.E], v.rearrange("(k e) -> k e", k=1).to_broadcast([P, s.E])).then_inc(all_in, 16)
                sp.wait_ge(consts, 1)
                z = 8
                sums = io.sums.rearrange("(c k p) n -> c p k n", k=z, p=P)
                for c in range(ET // z):
                    sp.dma_start(sums[c], zeros[:, :, :].to_broadcast([P, z, s.D])).then_inc(zeroed, 16)
                sp.wait_ge(zeroed, 16 * (ET // z))

            @block.vector
            def _(dve):
                done = [0]

                def then(ins):
                    done[0] += 1
                    ins.then_inc(step, 1)
                    dve.wait_ge(step, done[0])

                nc.vector.memset(rows_i[:, 0, :], 0)
                nc.vector.memset(rows_i[:, 1, :], s.PAD_DST).then_inc(cleared, 1)
                nc.vector.memset(src_all[:, s.E:], 0)
                nc.vector.memset(dst_all[:, s.E:], s.PAD_DST).then_inc(cleared, 1)
                nc.vector.memset(cum[:, 0, :], 0.0)
                dve.wait_ge(rows_in, 64)
                nc.vector.tensor_single_scalar(rows_w[:, 0, :], rows_i[:, 1, :], P - 1, ALU.bitwise_and)
                nc.vector.tensor_single_scalar(rows_w[:, 1, :], rows_i[:, 1, :], 7, ALU.arith_shift_right)
                then(nc.vector.tensor_single_scalar(rows_w[:, 2, :], rows_i[:, 0, :], 7, ALU.arith_shift_right))
                nc.vector.tensor_copy(rows_f[:, 0:2, :], rows_i[:, :, :])
                nc.vector.tensor_copy(rows_f[:, 2:5, :], rows_w[:, :, :]).then_inc(rows_ready, 1)
                dve.wait_ge(cols_ps, 1)
                then(nc.vector.tensor_copy(cols[:, :, :], ps_misc[:, 0:5 * ET].rearrange("p (v k) -> p v k", v=5)))
                nc.vector.tensor_copy(keep.dst_col[:, :], cols[:, 1, :])
                nc.vector.tensor_copy(keep.src_idx[:, :], cols[:, 0, :])
                dve.wait_ge(consts, 2)

                def one_hot(out, iota, col, n):
                    return nc.vector.tensor_tensor(out[:, :, :], iota[:, :, :].to_broadcast([P, ET, n]),
                                                   col.unsqueeze(2).to_broadcast([P, ET, n]), ALU.is_equal)

                one_hot(hot_low, iota_b, cols[:, 2, :], P)
                one_hot(hot_dst, iota_a, cols[:, 3, :], A).then_inc(hot_ready, 1)
                one_hot(hot_src, iota_a, cols[:, 4, :], A)
                dve.wait_ge(all_in, 32)
                then(nc.vector.tensor_copy(keep.dst_row[:, :], dst_all[:, :]))
                nc.vector.tensor_single_scalar(dst_all[:, :], dst_all[:, :], P - 1, ALU.bitwise_and)
                then(nc.vector.tensor_single_scalar(src_all[:, :], src_all[:, :], P - 1, ALU.bitwise_and))
                nc.vector.tensor_single_scalar(low_dst[:, :], dst_all[:, :], iota_p[:, 0:1], ALU.is_equal)
                nc.vector.tensor_single_scalar(low_src[:, :], src_all[:, :], iota_p[:, 0:1], ALU.is_equal)
                dve.wait_ge(hist_ready, 1)
                for q in range(EP):
                    then(nc.vector.tensor_tensor(cum[:, q + 1, :], cum[:, q, :],
                                                 ps_hist[q // 6][:, q % 6 * A:(q % 6 + 1) * A], ALU.add))
                nc.vector.tensor_scalar_add(scan[:, 0, :], cum[:, EP, :], 1.0).then_inc(deg_ready, 1)
                then(nc.vector.tensor_single_scalar(has[:, :], cum[:, EP, :], 0.5, ALU.is_gt))
                dve.wait_ge(std_ready, 1)
                then(nc.vector.reciprocal(keep.dinv[:, :], std[:, :]))
                nc.vector.tensor_tensor(keep.dinv2[:, :], keep.dinv[:, :], keep.dinv[:, :], ALU.mult)
                nc.vector.tensor_tensor(keep.has_dinv[:, :], keep.dinv[:, :], has[:, :], ALU.mult)
                then(nc.vector.tensor_copy(scan[:, 0, :], has[:, :]))
                shift, at = 1, 0
                while shift < A:
                    nc.vector.tensor_copy(scan[:, 1 - at, 0:shift], scan[:, at, 0:shift])
                    then(nc.vector.tensor_tensor(scan[:, 1 - at, shift:A], scan[:, at, shift:A],
                                                 scan[:, at, 0:A - shift], ALU.add))
                    shift, at = 2 * shift, 1 - at
                nc.vector.tensor_copy(junk[:, 0:1], scan[:, at, A - 1:A]).then_inc(rowsum_ready, 1)
                then(nc.vector.tensor_tensor(slot[:, :], scan[:, at, :], has[:, :], ALU.subtract))
                dve.wait_ge(base_ready, 1)
                then(nc.vector.tensor_copy(std[:, 0:1], ps_misc[:, 256:257]))
                then(nc.vector.tensor_single_scalar(slot[:, :], slot[:, :], std[:, 0:1], ALU.add))
                then(nc.vector.tensor_scalar(scan[:, 0, :], has[:, :], -float(s.SKIP), float(s.SKIP), ALU.mult, ALU.add))
                then(nc.vector.tensor_tensor(keep.node_idx[:, :], slot[:, :], scan[:, 0, :], ALU.add))
                nc.vector.memset(junk[:, 0:1], 0.0).then_inc(table_ready, 1)
                for n, (g0, g1) in enumerate(groups):
                    dve.wait_ge(picks_ps, n + 1)
                    m = g1 - g0
                    for v, hot in ((0, hot_dst), (1, hot_dst), (2, hot_src)):
                        r = nc.vector.tensor_tensor(
                            prod[:, v, 0:m, :], pick_banks[n % 2][v][:, 0:m * A].rearrange("p (k a) -> p k a", a=A),
                            hot[:, g0:g1, :], ALU.mult)
                        if v == 2:
                            r.then_inc(picks_read, 1)
                    dve.wait_ge(picks_read, n + 1)
                    for v in range(3):
                        r = nc.vector.tensor_reduce(picked[:, v, g0:g1], prod[:, v, 0:m, :], AX.X, ALU.add)
                    then(r)
                for k in range(ET):
                    q, i = k // 2, k % 2
                    then(nc.vector.scalar_tensor_tensor(
                        out=junk[:, :], in0=keep.dst_row[:, 2 * P * q:2 * P * (q + 1)], scalar=keep.dst_col[:, k:k + 1],
                        in1=earlier[:, i, :], op0=ALU.is_equal, op1=ALU.mult, accum_out=count[:, k:k + 1]))
                nc.vector.tensor_copy(keep.dinv_src[:, :], picked[:, 2, :])
                then(nc.vector.tensor_single_scalar(keep.has_prev[:, :], picked[:, 0, :], 0.5, ALU.is_gt))
                nc.vector.tensor_scalar(sel[:, :], keep.has_prev[:, :], -float(s.SKIP), float(s.SKIP), ALU.mult, ALU.add)
                then(nc.vector.tensor_scalar(sel2[:, :], count[:, :], 0.5, float(s.SKIP), ALU.is_gt, ALU.mult))
                nc.vector.tensor_tensor(keep.prev_idx[:, :], picked[:, 1, :], sel[:, :], ALU.add)
                then(nc.vector.tensor_tensor(sel2[:, :], sel2[:, :], picked[:, 1, :], ALU.add))
                then(nc.vector.tensor_scalar(sel[:, :], keep.dst_col[:, :], float(s.PAD_DST) - 0.5, float(s.SKIP),
                                             ALU.is_gt, ALU.mult))
                then(nc.vector.tensor_tensor(keep.sum_idx[:, :], sel[:, :], sel2[:, :], ALU.add))

            @block.scalar
            def _(act):
                act.wait_ge(deg_ready, 1)
                nc.scalar.activation(std[:, :], scan[:, 0, :], ACT.Sqrt).then_inc(std_ready, 1)

            @block.tensor
            def _(pe):
                pe.wait_ge(consts, 2)
                pe.wait_ge(rows_ready, 1)
                for v in range(5):
                    r = nc.tensor.transpose(ps_misc[:, v * ET:(v + 1) * ET], rows_f[:, v, :], keep.ident[0:ET, 0:ET])
                r.then_inc(cols_ps, 1)
                pe.wait_ge(hot_ready, 1)
                for k in range(ET):
                    q = k // 2
                    r = nc.tensor.matmul(ps_hist[q // 6][:, q % 6 * A:(q % 6 + 1) * A], hot_low[:, k, :], hot_dst[:, k, :],
                                         start=k % 2 == 0, stop=k % 2 == 1)
                r.then_inc(hist_ready, 1)
                pe.wait_ge(rowsum_ready, 1)
                nc.tensor.matmul(ps_misc[:, 256:257], below[:, :], junk[:, 0:1], start=True, stop=True).then_inc(base_ready, 1)
                pe.wait_ge(table_ready, 1)
                for n, (g0, g1) in enumerate(groups):
                    if n >= 2:
                        pe.wait_ge(picks_read, n - 1)
                    b = pick_banks[n % 2]
                    for k in range(g0, g1):
                        at = slice((k - g0) * A, (k - g0 + 1) * A)
                        e = slice(k * P, (k + 1) * P)
                        nc.tensor.matmul(b[0][:, at], low_dst[:, e], cum[:, k // 2, :], start=True, stop=True)
                        nc.tensor.matmul(b[1][:, at], low_dst[:, e], slot[:, :], start=True, stop=True)
                        r = nc.tensor.matmul(b[2][:, at], low_src[:, e], keep.dinv[:, :], start=True, stop=True)
                    r.then_inc(picks_ps, 1)


def message_sums(nc, s, layer, io, keep, mk, pieces, rows):
    ctx = ExitStack()
    tag = f"m{layer}_"
    with ctx:
        def sb(name, shape, dt=F32):
            return ctx.enter_context(nc.sbuf_tensor(tag + name, shape, dt))

        def sem(name):
            return mk.enter_context(nc.semaphore(tag + name))

        D, H, EP = s.D, s.H, s.EP
        NB = 4
        z = sb("z", [P, NB, D])
        pe_rows = sb("pe_rows", [P, NB, D]) if layer == 1 else None
        prev = sb("prev", [P, 2, D])
        same = sb("same", [P, 2, 2, 2 * P])
        g_idx = sb("g_idx", [P, NB], I32)
        p_idx = sb("p_idx", [P, 2], I32)
        s_idx = sb("s_idx", [P, 2], I32)
        stats = sb("stats", [P, NB, 2, 6])
        mv = sb("mv", [P, NB, 2])
        std = sb("std", [P, NB])
        rstd = sb("rstd", [P, NB])
        scale = sb("scale", [P, NB])
        shift = sb("shift", [P, NB])
        eps = sb("eps", [P, 1])
        stage = sb("stage", [P, 2, D])
        ps = [[ctx.enter_context(nc.psum_tensor(f"{tag}ps{j}{i}", [P, 2, H], F32)) for i in range(2)] for j in range(2)]

        ready = sem("ready")
        rows_in = sem("rows_in")
        col_sums = sem("col_sums")
        w_in = [sem(f"w_in{i}") for i in range(2)]
        w_hi = sem("w_hi")
        w_lo = sem("w_lo")
        z_in = [sem(f"z_in{b}") for b in range(NB)]
        pe_in = [sem(f"pe_in{b}") for b in range(NB)]
        idx_step = sem("idx_step")
        pool_gate = sem("pool_gate")
        dve_gate = sem("dve_gate")
        ln_dve = sem("ln_dve")
        std_ready = sem("std_ready")
        z_norm = sem("z_norm")
        times_a = sem("times_a")
        scaled = sem("scaled")
        msg_ready = sem("msg_ready")
        same_ready = sem("same_ready")
        summed = sem("summed")
        prev_in = [sem(f"prev_in{i}") for i in range(2)]
        sums_ready = sem("sums_ready")
        sums_out = [sem(f"sums_out{i}") for i in range(2)]
        bn_step = sem("bn_step")

        rows_src = io.x if layer == 1 else io.h1
        last_row = s.N - 1

        def staged_as(n, w):
            t = stage[:, n % 2, :]
            return t.rearrange("p (c n) -> p c n", n=w.shape[-1]) if len(w.shape) == 3 else t

        offset = bass.IndirectOffsetOnAxis

        with nc.Block() as block:
            @block.sync
            def _(sp):
                for row, t in rows:
                    n = row.shape[0]
                    sp.dma_start(t[:, :], row.rearrange("(k n) -> k n", k=1).to_broadcast([P, n])).then_inc(rows_in, 16)
                for n, (w, _hi, _lo) in enumerate(pieces):
                    if n >= 2:
                        sp.wait_ge(w_lo, n - 1)
                    sp.dma_start(staged_as(n, w), w).then_inc(w_in[n % 2], 16)
                sp.wait_ge(rows_in, 16 * len(rows))

            @block.gpsimd
            def _(pool):
                pool.sem_inc(summed, 2)
                pool.sem_inc(sums_ready, 4)
                pool.memset(prev[:, :, :], 0.0)
                pool.memset(eps[:, :], EPS).then_inc(ready, 1)
                if layer == 2:
                    pool.wait_ge(bn_step, 9)
                staged = [0]

                def gather_rows(k, b, pair, n):
                    pool.wait_ge(summed, pair + 1)
                    pool.sem_inc(pool_gate, 1)
                    pool.tensor_copy(g_idx[:, b:b + 1], keep.src_idx[:, bass.ds(k, 1)]).then_inc(idx_step, 1)
                    pool.wait_ge(idx_step, n + 1)
                    pool.sem_inc(pool_gate, 1)
                    pool.indirect_dma_start(z[:, b, :], None, rows_src, offset(ap=g_idx[:, b:b + 1], axis=0),
                                            bounds_check=last_row, oob_is_err=False).then_inc(z_in[b], 16)
                    if layer == 1:
                        pool.indirect_dma_start(pe_rows[:, b, :], None, io.pe, offset(ap=g_idx[:, b:b + 1], axis=0),
                                                bounds_check=last_row, oob_is_err=False).then_inc(pe_in[b], 16)

                def update_sums(q, n):
                    if not isinstance(q, int) or q > 0:
                        for i in range(2):
                            pool.wait_ge(sums_out[i], 16 * q)
                        pool.sem_inc(pool_gate, 1)
                    for i in range(2):
                        r = pool.tensor_copy(p_idx[:, i:i + 1], keep.prev_idx[:, bass.ds(2 * q + i, 1)])
                        r = pool.tensor_copy(s_idx[:, i:i + 1], keep.sum_idx[:, bass.ds(2 * q + i, 1)])
                    r.then_inc(idx_step, 1)
                    pool.wait_ge(idx_step, n + 1)
                    pool.sem_inc(pool_gate, 1)
                    for i in range(2):
                        pool.indirect_dma_start(prev[:, i, :], None, io.sums, offset(ap=p_idx[:, i:i + 1], axis=0),
                                                bounds_check=s.EPAD - 1, oob_is_err=False).then_inc(prev_in[i], 16)
                    for i in range(2):
                        pool.wait_ge(sums_ready, 2 * q + i + 5)
                        pool.sem_inc(pool_gate, 1)
                        pool.indirect_dma_start(io.sums, offset(ap=s_idx[:, i:i + 1], axis=0), prev[:, i, :], None,
                                                bounds_check=s.EPAD - 1, oob_is_err=False).then_inc(sums_out[i], 16)

                for i in range(2):
                    gather_rows(i, i, 0, i)
                for i in range(2):
                    gather_rows(2 + i, 2 + i, 1, 2 + i)
                update_sums(0, 4)
                with pool.Fori(0, EP // 2 - 1) as it:
                    for par in range(2):
                        q = 2 * it + 1 + par
                        for i in range(2):
                            gather_rows(2 * q + 2 + i, 2 * par + i, q + 1, 3 * q + 2 + i)
                        update_sums(q, 3 * q + 4)
                update_sums(EP - 1, 3 * EP - 1)
                for i in range(2):
                    pool.wait_ge(sums_out[i], 16 * EP)

            @block.scalar
            def _(act):
                for n, (_w, hi, _lo) in enumerate(pieces):
                    act.wait_ge(w_in[n % 2], 16 * (n // 2 + 1))
                    nc.scalar.copy(hi, staged_as(n, _w)).then_inc(w_hi, 1)
                if layer == 1:
                    act.wait_ge(ready, 1)
                else:
                    act.wait_ge(ready, 1)
                    act.wait_ge(bn_step, 4)
                    nc.scalar.activation(z[:, 2, :], z[:, 2, :], ACT.Sqrt, bias=eps[:, 0:1]).then_inc(bn_step, 1)

                def tile(k, b, k4):
                    if layer == 1:
                        act.wait_ge(ln_dve, 5 * k + 2)
                        nc.scalar.activation(std[:, b:b + 1], mv[:, b, 1:2], ACT.Sqrt, bias=eps[:, 0:1]).then_inc(std_ready, 1)
                        act.wait_ge(ln_dve, 5 * k + 5)
                        nc.scalar.activation(z[:, b, :], z[:, b, :], ACT.Identity, scale=scale[:, b:b + 1],
                                             bias=shift[:, b:b + 1]).then_inc(z_norm, 1)
                    else:
                        act.wait_ge(scaled, k + 1)
                        nc.scalar.activation(z[:, b, :], z[:, b, :], ACT.Relu, scale=scale[:, b:b + 1]).then_inc(msg_ready, 1)

                with act.Fori(0, EP // 2) as it:
                    for b in range(NB):
                        tile(NB * it + b, b, it + 1)

            @block.vector
            def _(dve):
                for n, (_w, hi, lo) in enumerate(pieces):
                    dve.wait_ge(w_hi, n + 1)
                    nc.vector.tensor_tensor(lo, staged_as(n, _w), hi.bitcast(F32), ALU.subtract).then_inc(w_lo, 1)
                if layer == 2:
                    mean, t, var = z[:, 0, :], z[:, 1, :], z[:, 2, :]
                    dve.wait_ge(rows_in, 16 * len(rows))
                    dve.wait_ge(col_sums, 1)
                    for j in range(2):
                        at = slice(j * H, (j + 1) * H)
                        nc.vector.tensor_single_scalar(mean[:, at], ps[0][0][:, j, :], 1.0 / s.N, ALU.mult)
                        r = nc.vector.tensor_single_scalar(var[:, at], ps[0][1][:, j, :], 1.0 / s.N, ALU.mult)
                    r.then_inc(bn_step, 1)
                    dve.wait_ge(bn_step, 1)
                    nc.vector.tensor_tensor(t, mean, mean, ALU.mult).then_inc(bn_step, 1)
                    dve.wait_ge(bn_step, 2)
                    nc.vector.tensor_tensor(var, var, t, ALU.subtract).then_inc(bn_step, 1)
                    dve.wait_ge(bn_step, 3)
                    nc.vector.tensor_single_scalar(var, var, 0.0, ALU.max).then_inc(bn_step, 1)
                    dve.wait_ge(bn_step, 5)
                    nc.vector.reciprocal(t, var).then_inc(bn_step, 1)
                    dve.wait_ge(bn_step, 6)
                    nc.vector.tensor_tensor(keep.bn_a[:, :], keep.bn_a[:, :], t, ALU.mult).then_inc(bn_step, 1)
                    dve.wait_ge(bn_step, 7)
                    nc.vector.tensor_tensor(t, keep.bn_a[:, :], mean, ALU.mult).then_inc(bn_step, 1)
                    dve.wait_ge(bn_step, 8)
                    nc.vector.tensor_tensor(keep.bn_b[:, :], keep.bn_b[:, :], t, ALU.subtract).then_inc(bn_step, 1)
                    dve.wait_ge(bn_step, 9)
                else:
                    dve.wait_ge(ready, 1)

                def message(k, b, use):
                    dve.wait_ge(z_in[b], 16 * use)
                    if layer == 1:
                        nc.vector.bn_stats(stats[:, b, 0, :], z[:, b, 0:H])
                        nc.vector.bn_stats(stats[:, b, 1, :], z[:, b, H:D]).then_inc(ln_dve, 1)
                        dve.wait_ge(ln_dve, 5 * k + 1)
                        dve.sem_inc(dve_gate, 1)
                        nc.vector.bn_aggr(mv[:, b, :], stats[:, b, :, :]).then_inc(ln_dve, 1)
                        dve.wait_ge(std_ready, k + 1)
                        nc.vector.reciprocal(rstd[:, b:b + 1], std[:, b:b + 1]).then_inc(ln_dve, 1)
                        dve.wait_ge(ln_dve, 5 * k + 3)
                        nc.vector.tensor_tensor(scale[:, b:b + 1], rstd[:, b:b + 1], keep.dinv_src[:, bass.ds(k, 1)],
                                                ALU.mult).then_inc(ln_dve, 1)
                        dve.wait_ge(ln_dve, 5 * k + 4)
                        nc.vector.tensor_scalar(shift[:, b:b + 1], mv[:, b, 0:1], scale[:, b:b + 1], -1.0,
                                                ALU.mult, ALU.mult).then_inc(ln_dve, 1)
                    else:
                        nc.vector.tensor_tensor(scale[:, b:b + 1], keep.dinv_src[:, bass.ds(k, 1)], keep.one[:, 0:1], ALU.mult)
                        nc.vector.tensor_tensor(z[:, b, :], z[:, b, :], keep.bn_a[:, :], ALU.mult).then_inc(times_a, 1)
                        dve.wait_ge(times_a, k + 1)
                        nc.vector.tensor_tensor(z[:, b, :], z[:, b, :], keep.bn_b[:, :], ALU.add).then_inc(scaled, 1)

                def message_pe(k, b, use):
                    dve.wait_ge(pe_in[b], 16 * use)
                    dve.wait_ge(z_norm, k + 1)
                    nc.vector.scalar_tensor_tensor(out=z[:, b, :], in0=pe_rows[:, b, :], scalar=keep.dinv_src[:, bass.ds(k, 1)],
                                                   in1=z[:, b, :], op0=ALU.mult, op1=ALU.add).then_inc(msg_ready, 1)

                def equality(q, par):
                    dve.wait_ge(summed, q + 1)
                    for i in range(2):
                        r = nc.vector.tensor_scalar(same[:, par, i, :], keep.dst_row[:, bass.ds(2 * P * q, 2 * P)],
                                                    keep.dst_col[:, bass.ds(2 * q + i, 1)], None, ALU.is_equal)
                    r.then_inc(same_ready, 1)

                def new_sums(q, par):
                    dve.wait_ge(summed, q + 3)
                    for i in range(2):
                        dve.wait_ge(prev_in[i], 16 * q + 16)
                        r = nc.vector.scalar_tensor_tensor(
                            out=prev[:, i, :], in0=prev[:, i, :], scalar=keep.has_prev[:, bass.ds(2 * q + i, 1)],
                            in1=ps[par][i][:, :, :].rearrange("p a n -> p (a n)"), op0=ALU.mult, op1=ALU.add)
                        r.then_inc(sums_ready, 1)

                def pair(q, par, use):
                    equality(q, par)
                    for i in range(2):
                        message(2 * q + i, 2 * par + i, use)
                    if layer == 1:
                        for i in range(2):
                            message_pe(2 * q + i, 2 * par + i, use)

                pair(0, 0, 1)
                pair(1, 1, 1)
                new_sums(0, 0)
                with dve.Fori(0, EP // 2 - 1) as it:
                    pair(2 * it + 2, 0, it + 2)
                    new_sums(2 * it + 1, 1)
                    pair(2 * it + 3, 1, it + 2)
                    new_sums(2 * it + 2, 0)
                new_sums(EP - 1, 1)

            @block.tensor
            def _(pe):
                if layer == 2:
                    for t, n in ((keep.acc, 0), (keep.acc2, 1)):
                        for j in range(2):
                            r = nc.tensor.matmul(ps[0][n][:, j, :], keep.ones[:, :], t[:, j * H:(j + 1) * H],
                                                 start=True, stop=True)
                    r.then_inc(col_sums, 1)
                    pe.wait_ge(bn_step, 1)

                def pair(q, par):
                    pe.wait_ge(same_ready, q + 1)
                    pe.wait_ge(msg_ready, 2 * q + 2)
                    pe.wait_ge(sums_ready, 2 * q + 2)
                    for j in range(2):
                        for h in range(2):
                            for i in range(2):
                                r = nc.tensor.matmul(ps[par][j][:, h, :], same[:, par, i, j * P:(j + 1) * P],
                                                     z[:, 2 * par + i, h * H:(h + 1) * H], start=i == 0, stop=i == 1)
                    r.then_inc(summed, 1)

                with pe.Fori(0, EP // 2) as it:
                    for par in range(2):
                        pair(2 * it + par, par)


def conv1(nc, s, io, keep, mk):
    ctx = ExitStack()
    with ctx:
        def sb(name, shape, dt=F32):
            return ctx.enter_context(nc.sbuf_tensor("c1_" + name, shape, dt))

        def sem(name):
            return mk.enter_context(nc.semaphore("c1_" + name))

        D, H, KD, NT, LAST = s.D, s.H, s.KD, s.NT, s.LAST
        xt = sb("xt", [P, 2, D])
        pt = sb("pt", [P, 2, D])
        et = sb("et", [P, 2, D])
        y = sb("y", [P, 2, D])
        y_hi = sb("y_hi", [P, 2, KD, P], F32R)
        y_lo = sb("y_lo", [P, 2, KD, P], F32R)
        ht = sb("ht", [P, 2, D])
        sq = sb("sq", [P, D])
        e_idx = sb("e_idx", [P, 2], I32)
        stats = sb("stats", [P, 2, 2, 6])
        mv = sb("mv", [P, 2, 2])
        small = sb("small", [P, 2, 4])
        eps = sb("eps", [P, 1])
        ps_t = [ctx.enter_context(nc.psum_tensor(f"c1_t{i}", [P, KD, P], F32)) for i in range(2)]
        ps_u = [ctx.enter_context(nc.psum_tensor(f"c1_u{h}", [P, H], F32)) for h in range(2)]

        ready = sem("ready")
        x_in = [sem(f"x_in{i}") for i in range(2)]
        pe_in = [sem(f"pe_in{i}") for i in range(2)]
        e_in = [sem(f"e_in{i}") for i in range(2)]
        idx_step = sem("idx_step")
        pool_gate = sem("pool_gate")
        dve_gate = sem("dve_gate")
        ln_dve = sem("ln_dve")
        std_ready = sem("std_ready")
        normed = sem("normed")
        with_pe = sem("with_pe")
        y_ready = sem("y_ready")
        transposed = sem("transposed")
        hi_ready = sem("hi_ready")
        lo_ready = sem("lo_ready")
        products = sem("products")
        h_ready = sem("h_ready")
        added = sem("added")
        squared = sem("squared")
        sq_added = sem("sq_added")
        h_out = [sem(f"h_out{i}") for i in range(2)]

        rows = lambda t: P if not isinstance(t, int) or t < NT - 1 else LAST
        block_rows = lambda ap, t: ap[bass.ds(t * P, rows(t)), :]
        MAIN = NT - 3
        offset = bass.IndirectOffsetOnAxis

        with nc.Block() as block:
            @block.sync
            def _(sp):
                def loads(t, par, use):
                    sp.wait_ge(normed, t + 1)
                    sp.dma_start(xt[0:rows(t), par, :], block_rows(io.x, t)).then_inc(x_in[par], 16)
                    sp.wait_ge(with_pe, t + 1)
                    sp.dma_start(pt[0:rows(t), par, :], block_rows(io.pe, t)).then_inc(pe_in[par], 16)

                def store(t, par):
                    sp.wait_ge(h_ready, 2 * t + 4)
                    sp.dma_start(block_rows(io.h1, t), ht[0:rows(t), par, :]).then_inc(h_out[par], 16)

                sp.wait_ge(ready, 1)
                loads(0, 0, 1)
                loads(1, 1, 1)
                with sp.Fori(0, MAIN // 2) as it:
                    for par in range(2):
                        t = 2 * it + par
                        loads(t + 2, par, it + 2)
                        store(t, par)
                for t in range(MAIN, NT):
                    if t + 2 < NT:
                        loads(t + 2, t % 2, None)
                    store(t, t % 2)
                for par in range(2):
                    sp.wait_ge(h_out[par], 16 * ((NT + 1 - par) // 2) + 16)

            @block.gpsimd
            def _(pool):
                for v, n in ((normed, 2), (with_pe, 2), (y_ready, 2), (transposed, 2), (lo_ready, 2), (products, 4),
                             (h_ready, 2), (added, 2), (squared, 2), (sq_added, 1), (h_out[0], 16), (h_out[1], 16)):
                    pool.sem_inc(v, n)
                pool.memset(et[:, :, :], 0.0)
                pool.memset(keep.acc[:, :], 0.0)
                pool.memset(keep.acc2[:, :], 0.0)
                pool.memset(eps[:, :], EPS).then_inc(ready, 1)
                pool.wait_ge(ready, 1)

                def gather(t, par):
                    pool.wait_ge(y_ready, t + 1)
                    pool.sem_inc(pool_gate, 1)
                    pool.tensor_copy(e_idx[:, par:par + 1], keep.node_idx[:, bass.ds(t, 1)]).then_inc(idx_step, 1)
                    pool.wait_ge(idx_step, t + 1)
                    pool.sem_inc(pool_gate, 1)
                    pool.indirect_dma_start(et[:, par, :], None, io.sums, offset(ap=e_idx[:, par:par + 1], axis=0),
                                            bounds_check=s.EPAD - 1, oob_is_err=False).then_inc(e_in[par], 16)

                def add_squares(t, n):
                    pool.wait_ge(squared, t + 3)
                    pool.sem_inc(pool_gate, 1)
                    pool.tensor_tensor(keep.acc2[0:n, :], keep.acc2[0:n, :], sq[0:n, :], ALU.add).then_inc(sq_added, 1)

                gather(0, 0)
                gather(1, 1)
                with pool.Fori(0, MAIN // 2) as it:
                    for par in range(2):
                        t = 2 * it + par
                        gather(t + 2, par)
                        pool.wait_ge(sq_added, t + 1)
                        add_squares(t, P)
                for t in range(MAIN, NT):
                    if t + 2 < NT:
                        gather(t + 2, t % 2)
                    pool.wait_ge(sq_added, t + 1)
                    add_squares(t, rows(t))

            @block.scalar
            def _(act):
                def norm(t, par):
                    act.wait_ge(ln_dve, 5 * t + 2)
                    nc.scalar.activation(small[:, par, 0:1], mv[:, par, 1:2], ACT.Sqrt, bias=eps[:, 0:1]).then_inc(std_ready, 1)
                    act.wait_ge(transposed, t + 1)
                    act.wait_ge(ln_dve, 5 * t + 5)
                    nc.scalar.activation(y[:, par, :], xt[:, par, :], ACT.Identity, scale=small[:, par, 2:3],
                                         bias=small[:, par, 3:4]).then_inc(normed, 1)

                def split_hi(t, par):
                    act.wait_ge(transposed, t + 3)
                    act.wait_ge(products, 2 * t + 2)
                    nc.scalar.copy(y_hi[:, par, :, :], ps_t[par][:, :, :]).then_inc(hi_ready, 1)

                def square(t, par):
                    act.wait_ge(h_ready, 2 * t + 4)
                    act.wait_ge(sq_added, t + 1)
                    nc.scalar.activation(sq[:, :], ht[:, par, :], ACT.Square).then_inc(squared, 1)

                act.wait_ge(ready, 1)
                norm(0, 0)
                norm(1, 1)
                split_hi(0, 0)
                with act.Fori(0, MAIN // 2) as it:
                    for par in range(2):
                        t = 2 * it + par
                        split_hi(t + 1, 1 - par)
                        norm(t + 2, par)
                        square(t, par)
                for t in range(MAIN, NT):
                    if t + 1 < NT:
                        split_hi(t + 1, (t + 1) % 2)
                    if t + 2 < NT:
                        norm(t + 2, t % 2)
                    square(t, t % 2)

            @block.vector
            def _(dve):
                def rows_of(t, par, use):
                    dve.wait_ge(x_in[par], 16 * use)
                    nc.vector.bn_stats(stats[:, par, 0, :], xt[:, par, 0:H])
                    nc.vector.bn_stats(stats[:, par, 1, :], xt[:, par, H:D]).then_inc(ln_dve, 1)
                    dve.wait_ge(ln_dve, 5 * t + 1)
                    dve.sem_inc(dve_gate, 1)
                    nc.vector.bn_aggr(mv[:, par, :], stats[:, par, :, :]).then_inc(ln_dve, 1)
                    dve.wait_ge(std_ready, t + 1)
                    nc.vector.reciprocal(small[:, par, 1:2], small[:, par, 0:1]).then_inc(ln_dve, 1)
                    dve.wait_ge(ln_dve, 5 * t + 3)
                    nc.vector.tensor_tensor(small[:, par, 2:3], small[:, par, 1:2], keep.dinv2[:, bass.ds(t, 1)],
                                            ALU.mult).then_inc(ln_dve, 1)
                    dve.wait_ge(ln_dve, 5 * t + 4)
                    nc.vector.tensor_scalar(small[:, par, 3:4], mv[:, par, 0:1], small[:, par, 2:3], -1.0,
                                            ALU.mult, ALU.mult).then_inc(ln_dve, 1)

                def rows_sum(t, par, use):
                    dve.wait_ge(pe_in[par], 16 * use)
                    dve.wait_ge(normed, t + 3)
                    nc.vector.scalar_tensor_tensor(out=y[:, par, :], in0=pt[:, par, :], scalar=keep.dinv2[:, bass.ds(t, 1)],
                                                   in1=y[:, par, :], op0=ALU.mult, op1=ALU.add).then_inc(with_pe, 1)
                    dve.wait_ge(e_in[par], 16 * use)
                    dve.wait_ge(with_pe, t + 3)
                    nc.vector.scalar_tensor_tensor(out=y[:, par, :], in0=et[:, par, :], scalar=keep.has_dinv[:, bass.ds(t, 1)],
                                                   in1=y[:, par, :], op0=ALU.mult, op1=ALU.add).then_inc(y_ready, 1)

                def split_lo(t, par):
                    dve.wait_ge(hi_ready, t + 1)
                    nc.vector.tensor_tensor(y_lo[:, par, :, :], ps_t[par][:, :, :], y_hi[:, par, :, :].bitcast(F32),
                                            ALU.subtract).then_inc(lo_ready, 1)

                def evacuate(t, par, use):
                    dve.wait_ge(h_out[par], 16 * use + 16)
                    dve.wait_ge(squared, t + 1)
                    dve.wait_ge(added, t + 2)
                    for h in range(2):
                        dve.wait_ge(products, 2 * t + h + 5)
                        nc.vector.tensor_tensor(ht[:, par, h * H:(h + 1) * H], ps_u[h][:, :], keep.b1[:, h * H:(h + 1) * H],
                                                ALU.add).then_inc(h_ready, 1)
                    n = rows(t)
                    dve.wait_ge(h_ready, 2 * t + 4)
                    nc.vector.tensor_tensor(keep.acc[0:n, :], keep.acc[0:n, :], ht[0:n, par, :], ALU.add).then_inc(added, 1)

                dve.wait_ge(ready, 1)
                rows_of(0, 0, 1)
                rows_sum(0, 0, 1)
                rows_of(1, 1, 1)
                rows_sum(1, 1, 1)
                split_lo(0, 0)
                with dve.Fori(0, MAIN // 2) as it:
                    for par in range(2):
                        t = 2 * it + par
                        split_lo(t + 1, 1 - par)
                        rows_of(t + 2, par, it + 2)
                        rows_sum(t + 2, par, it + 2)
                        evacuate(t, par, it)
                for t in range(MAIN, NT):
                    if t + 1 < NT:
                        split_lo(t + 1, (t + 1) % 2)
                    if t + 2 < NT:
                        rows_of(t + 2, t % 2, t // 2 + 2)
                        rows_sum(t + 2, t % 2, t // 2 + 2)
                    evacuate(t, t % 2, t // 2)

            @block.tensor
            def _(pe):
                def transposes(t, par):
                    pe.wait_ge(lo_ready, t + 1)
                    pe.wait_ge(y_ready, t + 3)
                    for k in range(KD):
                        r = nc.tensor.transpose(ps_t[par][:, k, :], y[:, par, k * P:(k + 1) * P], keep.ident[:, :])
                    r.then_inc(transposed, 1)

                def multiply(t, par):
                    pe.wait_ge(lo_ready, t + 3)
                    for h in range(2):
                        pe.wait_ge(h_ready, 2 * t + h + 1)
                        at = slice(h * H, (h + 1) * H)
                        for k in range(KD):
                            hi, lo = y_hi[:, par, k, :], y_lo[:, par, k, :]
                            nc.tensor.matmul(ps_u[h][:, :], hi, keep.w_hi[:, k, at], start=k == 0, stop=False)
                            nc.tensor.matmul(ps_u[h][:, :], hi, keep.w_lo[:, k, at], start=False, stop=False)
                            r = nc.tensor.matmul(ps_u[h][:, :], lo, keep.w_hi[:, k, at], start=False, stop=k == KD - 1)
                        r.then_inc(products, 1)

                pe.wait_ge(ready, 1)
                transposes(0, 0)
                with pe.Fori(0, MAIN // 2) as it:
                    for par in range(2):
                        t = 2 * it + par
                        transposes(t + 1, 1 - par)
                        multiply(t, par)
                for t in range(MAIN, NT):
                    if t + 1 < NT:
                        transposes(t + 1, (t + 1) % 2)
                    multiply(t, t % 2)


def conv2_ffn(nc, s, io, keep, mk):
    ctx = ExitStack()
    with ctx:
        def sb(name, shape, dt=F32):
            return ctx.enter_context(nc.sbuf_tensor("c2_" + name, shape, dt))

        def sem(name):
            return mk.enter_context(nc.semaphore("c2_" + name))

        D, H, KD, KF, F, NT, LAST = s.D, s.H, s.KD, s.KF, s.F, s.NT, s.LAST
        EX = 8
        ht = sb("ht", [P, 2, D])
        xt = sb("xt", [P, 2, D])
        et = sb("et", [P, 2, D])
        y_hi = sb("y_hi", [P, KD, P], F32R)
        y_lo = sb("y_lo", [P, KD, P], F32R)
        x2 = sb("x2", [P, 2, D])
        xn = sb("xn", [P, D])
        x_hi = sb("x_hi", [P, KD, P], F32R)
        x_lo = sb("x_lo", [P, KD, P], F32R)
        hid = sb("hid", [P, F])
        m_hi = sb("m_hi", [P, KF, P], F32R)
        m_lo = sb("m_lo", [P, KF, P], F32R)
        rw_f = xn[:, 0:KD * EX].rearrange("p (k e) -> p k e", e=EX)
        rw = sb("rw", [P, KD, 2, EX], F32R)
        fb2_f = x2[0:3 * EX, 0, :]
        fb2 = sb("fb2", [3 * EX, D], F32R)
        gate_t = sb("gate_t", [3 * EX, P], F32R)
        e_idx = sb("e_idx", [P, 2], I32)
        stats = sb("stats", [P, 2, 6])
        mv = sb("mv", [P, 2])
        small = sb("small", [P, 4])
        half_p = sb("half_p", [P, 2])
        log_b = sb("log_b", [P, EX])
        logit = sb("logit", [P, EX])
        top = sb("top", [P, EX])
        top_i = sb("top_i", [P, EX], U32)
        top_f = sb("top_f", [P, 2])
        diff = sb("diff", [P, 1])
        th = sb("th", [P, 1])
        prob = sb("prob", [P, 2])
        pick = sb("pick", [P, 2, EX])
        gate = sb("gate", [P, 1, EX])
        gate3 = sb("gate3", [P, 3, EX], F32R)
        mid = sb("mid", [3 * EX, 3])
        ps_t = ctx.enter_context(nc.psum_tensor("c2_t", [P, KD, P], F32))
        ps_u = [ctx.enter_context(nc.psum_tensor(f"c2_u{h}", [P, H], F32)) for h in range(2)]
        ps_v = [ctx.enter_context(nc.psum_tensor(f"c2_v{h}", [P, H], F32)) for h in range(2)]
        ps_f = ctx.enter_context(nc.psum_tensor("c2_f", [P, F], F32))
        ps_m = ctx.enter_context(nc.psum_tensor("c2_m", [P, KF, P], F32))
        ps_r = ps_m[:, 0, 0:2 * EX]
        ps_g = ps_f[0:3 * EX, 0:P]

        ready = sem("ready")
        rows_in = sem("rows_in")
        rest_in = sem("rest_in")
        set_up = sem("set_up")
        h_in = [sem(f"h_in{i}") for i in range(2)]
        x_in = [sem(f"x_in{i}") for i in range(2)]
        e_in = [sem(f"e_in{i}") for i in range(2)]
        idx_step = sem("idx_step")
        pool_gate = sem("pool_gate")
        dve_gate = sem("dve_gate")
        bn_dve = sem("bn_dve")
        y_ready = sem("y_ready")
        y_tr = sem("y_tr")
        y_hi_ready = sem("y_hi_ready")
        y_lo_ready = sem("y_lo_ready")
        conv = sem("conv")
        biased = sem("biased")
        res = sem("res")
        ln_dve = sem("ln_dve")
        pw = sem("pw")
        xn_ready = sem("xn_ready")
        x_tr = sem("x_tr")
        x_hi_ready = sem("x_hi_ready")
        x_lo_ready = sem("x_lo_ready")
        routed = sem("routed")
        up = sem("up")
        route_dve = sem("route_dve")
        th_ready = sem("th_ready")
        hid_bias = sem("hid_bias")
        hid_gelu = sem("hid_gelu")
        hid_ready = sem("hid_ready")
        m_tr = sem("m_tr")
        m_hi_ready = sem("m_hi_ready")
        m_lo_ready = sem("m_lo_ready")
        gate_ready = sem("gate_ready")
        down = sem("down")
        out_ready = sem("out_ready")
        out_sent = [sem(f"out_sent{i}") for i in range(2)]

        rows = lambda t: P if not isinstance(t, int) or t < NT - 1 else LAST
        block_rows = lambda ap, t: ap[bass.ds(t * P, rows(t)), :]
        MAIN = NT - 5
        offset = bass.IndirectOffsetOnAxis

        with nc.Block() as block:
            @block.sync
            def _(sp):
                def loads(t, par):
                    sp.wait_ge(y_tr, t + 1)
                    sp.dma_start(ht[0:rows(t), par, :], block_rows(io.h1, t)).then_inc(h_in[par], 16)
                    sp.wait_ge(res, 2 * t + 2)
                    sp.dma_start(xt[0:rows(t), par, :], block_rows(io.x, t)).then_inc(x_in[par], 16)

                def store(t, par):
                    sp.wait_ge(out_ready, 2 * t + 4)
                    sp.dma_start(block_rows(io.out, t), x2[0:rows(t), par, :]).then_inc(out_sent[par], 16)

                sp.wait_ge(ready, 1)
                loads(0, 0)
                loads(1, 1)
                for row, t in ((io.b2, keep.b2), (io.fb1, keep.fb1)):
                    n = row.shape[0]
                    sp.dma_start(t[:, :], row.rearrange("(k n) -> k n", k=1).to_broadcast([P, n])).then_inc(rows_in, 16)
                sp.dma_start(rw_f, io.rwt.rearrange("(k p) e -> p k e", p=P)).then_inc(rest_in, 16)
                for i in range(3):
                    sp.dma_start(fb2_f[i * EX:(i + 1) * EX, :], io.fb2).then_inc(rest_in, 16)
                loads(2, 0)
                with sp.Fori(0, MAIN // 2) as it:
                    for i in range(2):
                        t = 2 * it + 1 + i
                        loads(t + 2, 1 - i)
                        store(t - 1, i)
                for t in range(MAIN + 1, NT + 1):
                    if t + 2 < NT:
                        loads(t + 2, t % 2)
                    store(t - 1, (t - 1) % 2)
                for par in range(2):
                    sp.wait_ge(out_sent[par], 16 * ((NT + 1 - par) // 2) + 16)

            @block.gpsimd
            def _(pool):
                for v, n in ((y_ready, 2), (y_tr, 2), (conv, 2), (biased, 2), (res, 4), (x_tr, 1), (up, 1), (m_tr, 1),
                             (down, 2), (out_ready, 2), (out_sent[0], 16), (out_sent[1], 16)):
                    pool.sem_inc(v, n)
                pool.memset(et[:, :, :], 0.0)
                pool.memset(half_p[:, 0:1], -0.5)
                pool.memset(half_p[:, 1:2], EPS)
                pool.iota(mid[:, 0:1], pattern=[[0, 1]], base=0, channel_multiplier=1,
                          allow_small_or_imprecise_dtypes=True).then_inc(ready, 1)
                pool.wait_ge(ready, 1)

                def gather(t, par):
                    pool.wait_ge(y_ready, t + 1)
                    pool.sem_inc(pool_gate, 1)
                    pool.tensor_copy(e_idx[:, par:par + 1], keep.node_idx[:, bass.ds(t, 1)]).then_inc(idx_step, 1)
                    pool.wait_ge(idx_step, t + 1)
                    pool.sem_inc(pool_gate, 1)
                    pool.indirect_dma_start(et[:, par, :], None, io.sums, offset(ap=e_idx[:, par:par + 1], axis=0),
                                            bounds_check=s.EPAD - 1, oob_is_err=False).then_inc(e_in[par], 16)

                def root(t):
                    pool.wait_ge(ln_dve, 4 * t + 2)
                    pool.sem_inc(pool_gate, 1)
                    pool.tensor_tensor(small[:, 0:1], mv[:, 1:2], half_p[:, 1:2], ALU.add).then_inc(pw, 1)
                    pool.wait_ge(pw, 2 * t + 1)
                    pool.sem_inc(pool_gate, 1)
                    pool.tensor_tensor(small[:, 1:2], small[:, 0:1], half_p[:, 0:1], ALU.pow).then_inc(pw, 1)

                gather(0, 0)
                gather(1, 1)
                gather(2, 0)
                root(0)
                with pool.Fori(0, MAIN // 2) as it:
                    for i in range(2):
                        t = 2 * it + 1 + i
                        gather(t + 2, 1 - i)
                        root(t)
                for t in range(MAIN + 1, NT):
                    if t + 2 < NT:
                        gather(t + 2, t % 2)
                    root(t)

            @block.scalar
            def _(act):
                def y_split_hi(t):
                    act.wait_ge(y_tr, t + 3)
                    act.wait_ge(conv, 2 * t + 2)
                    nc.scalar.copy(y_hi[:, :, :], ps_t[:, :, :]).then_inc(y_hi_ready, 1)

                def norm(t, par):
                    act.wait_ge(x_tr, t + 1)
                    act.wait_ge(ln_dve, 4 * t + 4)
                    nc.scalar.activation(xn[:, :], x2[:, par, :], ACT.Identity, scale=small[:, 2:3],
                                         bias=small[:, 3:4]).then_inc(xn_ready, 1)

                def x_split_hi(t):
                    act.wait_ge(x_tr, t + 2)
                    act.wait_ge(up, t + 1)
                    nc.scalar.copy(x_hi[:, :, :], ps_t[:, :, :]).then_inc(x_hi_ready, 1)

                def route_and_gelu(t):
                    act.wait_ge(route_dve, 8 * t + 4)
                    nc.scalar.activation(th[:, :], diff[:, :], ACT.Tanh, scale=0.5).then_inc(th_ready, 1)
                    act.wait_ge(hid_bias, t + 1)
                    nc.scalar.activation(hid[:, :], hid[:, :], ACT.Gelu).then_inc(hid_gelu, 1)

                def m_split_hi(t):
                    act.wait_ge(m_tr, t + 2)
                    act.wait_ge(down, 2 * t + 2)
                    nc.scalar.copy(gate_t[:, :], ps_g).then_inc(gate_ready, 1)
                    nc.scalar.copy(m_hi[:, :, :], ps_m[:, :, :]).then_inc(m_hi_ready, 1)

                act.wait_ge(set_up, 1)
                nc.scalar.activation(th[:, :], mv[:, 0:1], ACT.Gelu)
                y_split_hi(0)
                y_split_hi(1)
                norm(0, 0)

                def step(t, par):
                    x_split_hi(t - 1)
                    route_and_gelu(t - 1)
                    m_split_hi(t - 1)

                def after(t, par):
                    y_split_hi(t + 1)
                    norm(t, par)

                with act.Fori(0, MAIN // 2) as it:
                    for i in range(2):
                        t = 2 * it + 1 + i
                        step(t, 1 - i)
                        y_split_hi(t + 1)
                        norm(t, 1 - i)
                for t in range(MAIN + 1, NT + 1):
                    step(t, t % 2)
                    if t + 1 < NT:
                        y_split_hi(t + 1)
                    if t < NT:
                        norm(t, t % 2)

            @block.vector
            def _(dve):
                dve.wait_ge(ready, 1)
                nc.vector.memset(mv[:, :], 0.0).then_inc(set_up, 1)
                dve.wait_ge(rest_in, 64)
                nc.vector.tensor_copy(rw[:, :, 0, :], rw_f)
                nc.vector.tensor_single_scalar(mid[:, 1:2], mid[:, 0:1], float(EX) - 0.5, ALU.is_gt)
                nc.vector.tensor_single_scalar(mid[:, 2:3], mid[:, 0:1], float(2 * EX) - 0.5, ALU.is_lt)
                nc.vector.tensor_copy(fb2[:, :], fb2_f).then_inc(set_up, 1)
                dve.wait_ge(set_up, 2)
                nc.vector.tensor_tensor(rw[:, :, 1, :], rw_f, rw[:, :, 0, :].bitcast(F32), ALU.subtract)
                nc.vector.tensor_tensor(mid[:, 1:2], mid[:, 1:2], mid[:, 2:3], ALU.mult)
                nc.vector.tensor_tensor(fb2_f, fb2_f, fb2[:, :].bitcast(F32), ALU.subtract).then_inc(set_up, 1)
                dve.wait_ge(set_up, 3)
                nc.vector.tensor_scalar(mid[:, 2:3], mid[:, 1:2], -1.0, 1.0, ALU.mult, ALU.add)
                nc.vector.tensor_single_scalar(fb2_f, fb2_f, mid[:, 1:2], ALU.mult).then_inc(set_up, 1)
                dve.wait_ge(set_up, 4)
                nc.vector.scalar_tensor_tensor(out=fb2[:, :], in0=fb2[:, :].bitcast(F32), scalar=mid[:, 2:3], in1=fb2_f,
                                               op0=ALU.mult, op1=ALU.add).then_inc(set_up, 1)
                dve.wait_ge(rows_in, 32)

                def conv_input(t, par, use):
                    dve.wait_ge(h_in[par], 16 * use)
                    nc.vector.tensor_tensor(ht[:, par, :], ht[:, par, :], keep.bn_a[:, :], ALU.mult).then_inc(bn_dve, 1)
                    dve.wait_ge(bn_dve, 3 * t + 1)
                    nc.vector.tensor_tensor(ht[:, par, :], ht[:, par, :], keep.bn_b[:, :], ALU.add).then_inc(bn_dve, 1)
                    dve.wait_ge(bn_dve, 3 * t + 2)
                    nc.vector.tensor_scalar(ht[:, par, :], ht[:, par, :], 0.0, keep.dinv2[:, bass.ds(t, 1)],
                                            ALU.max, ALU.mult).then_inc(bn_dve, 1)
                    dve.wait_ge(e_in[par], 16 * use)
                    dve.wait_ge(bn_dve, 3 * t + 3)
                    nc.vector.scalar_tensor_tensor(out=ht[:, par, :], in0=et[:, par, :], scalar=keep.has_dinv[:, bass.ds(t, 1)],
                                                   in1=ht[:, par, :], op0=ALU.mult, op1=ALU.add).then_inc(y_ready, 1)

                def y_split_lo(t):
                    dve.wait_ge(y_hi_ready, t + 1)
                    nc.vector.tensor_tensor(y_lo[:, :, :], ps_t[:, :, :], y_hi[:, :, :].bitcast(F32),
                                            ALU.subtract).then_inc(y_lo_ready, 1)

                def residual(t, par, use, h):
                    at = slice(h * H, (h + 1) * H)
                    if h == 0:
                        dve.wait_ge(out_sent[par], 16 * use)
                        dve.wait_ge(x_in[par], 16 * use)
                    dve.wait_ge(conv, 2 * t + h + 3)
                    nc.vector.tensor_tensor(x2[:, par, at], ps_u[h][:, :], keep.b2[:, at], ALU.add).then_inc(biased, 1)
                    dve.wait_ge(biased, 2 * t + h + 3)
                    nc.vector.scalar_tensor_tensor(out=x2[:, par, at], in0=x2[:, par, at], scalar=0.0, in1=xt[:, par, at],
                                                   op0=ALU.max, op1=ALU.add).then_inc(res, 1)
                    dve.wait_ge(res, 2 * t + h + 5)
                    r = nc.vector.bn_stats(stats[:, h, :], x2[:, par, at])
                    if h == 1:
                        r.then_inc(ln_dve, 1)

                def norm_constants(t):
                    dve.wait_ge(ln_dve, 4 * t + 1)
                    dve.sem_inc(dve_gate, 1)
                    nc.vector.bn_aggr(mv[:, :], stats[:, :, :]).then_inc(ln_dve, 1)
                    dve.wait_ge(pw, 2 * t + 2)
                    nc.vector.tensor_tensor(small[:, 2:3], small[:, 1:2], keep.one[:, 0:1], ALU.mult).then_inc(ln_dve, 1)
                    dve.wait_ge(ln_dve, 4 * t + 3)
                    nc.vector.tensor_scalar(small[:, 3:4], mv[:, 0:1], small[:, 2:3], -1.0,
                                            ALU.mult, ALU.mult).then_inc(ln_dve, 1)

                def x_split_lo(t):
                    dve.wait_ge(x_hi_ready, t + 1)
                    nc.vector.tensor_tensor(x_lo[:, :, :], ps_t[:, :, :], x_hi[:, :, :].bitcast(F32),
                                            ALU.subtract).then_inc(x_lo_ready, 1)

                def route(t):
                    base = 8 * t
                    dve.wait_ge(routed, t + 1)
                    nc.vector.tensor_copy(log_b[:, :], ps_r[:, EX:2 * EX]).then_inc(route_dve, 1)
                    dve.wait_ge(route_dve, base + 1)
                    nc.vector.tensor_tensor(logit[:, :], ps_r[:, 0:EX], log_b[:, :], ALU.add).then_inc(route_dve, 1)
                    dve.wait_ge(route_dve, base + 2)
                    dve.sem_inc(dve_gate, 1)
                    nc.vector.max(top[:, :], logit[:, :]).then_inc(route_dve, 1)
                    dve.wait_ge(route_dve, base + 3)
                    dve.sem_inc(dve_gate, 1)
                    nc.vector.max_index(top_i[:, :], top[:, :], logit[:, :])
                    nc.vector.tensor_tensor(diff[:, :], top[:, 0:1], top[:, 1:2], ALU.subtract).then_inc(route_dve, 1)
                    dve.wait_ge(route_dve, base + 4)
                    nc.vector.tensor_scalar(top_f[:, :], top_i[:, 0:2], 1.0, None, ALU.mult)
                    dve.wait_ge(th_ready, t + 1)
                    nc.vector.tensor_scalar(prob[:, 0:1], th[:, :], 0.5, 0.5, ALU.mult, ALU.add)
                    nc.vector.tensor_scalar(prob[:, 1:2], th[:, :], -0.5, 0.5, ALU.mult, ALU.add).then_inc(route_dve, 1)
                    dve.wait_ge(route_dve, base + 5)
                    for i in range(2):
                        r = nc.vector.tensor_scalar(pick[:, i, :], keep.iota_e[:, :], top_f[:, i:i + 1], prob[:, i:i + 1],
                                                    ALU.is_equal, ALU.mult)
                    r.then_inc(route_dve, 1)
                    dve.wait_ge(route_dve, base + 6)
                    nc.vector.tensor_tensor(gate[:, 0, :], pick[:, 0, :], pick[:, 1, :], ALU.add).then_inc(route_dve, 1)
                    dve.wait_ge(route_dve, base + 7)
                    dve.wait_ge(m_tr, t + 1)
                    nc.vector.tensor_tensor(gate3[:, 0:2, :], gate[:, :, :].to_broadcast([P, 2, EX]),
                                            keep.zero[:, 0:1].unsqueeze(2).to_broadcast([P, 2, EX]),
                                            ALU.add).then_inc(route_dve, 1)
                    dve.wait_ge(route_dve, base + 8)
                    nc.vector.tensor_tensor(gate3[:, 2, :], gate[:, 0, :], gate3[:, 0, :].bitcast(F32), ALU.subtract)

                def hidden(t):
                    dve.wait_ge(m_tr, t + 1)
                    dve.wait_ge(up, t + 2)
                    nc.vector.tensor_tensor(hid[:, :], ps_f[:, :], keep.fb1[:, :], ALU.add).then_inc(hid_bias, 1)

                def gated(t):
                    dve.wait_ge(hid_gelu, t + 1)
                    hid_e = hid[:, :].rearrange("p (e f) -> p e f", e=EX)
                    nc.vector.tensor_tensor(hid_e, hid_e, gate[:, 0, :].unsqueeze(2).to_broadcast([P, EX, F // EX]),
                                            ALU.mult).then_inc(hid_ready, 1)

                def m_split_lo(t):
                    dve.wait_ge(m_hi_ready, t + 1)
                    nc.vector.tensor_tensor(m_lo[:, :, :], ps_m[:, :, :], m_hi[:, :, :].bitcast(F32),
                                            ALU.subtract).then_inc(m_lo_ready, 1)

                def output(t, par):
                    dve.wait_ge(xn_ready, t + 1)
                    for h in range(2):
                        at = slice(h * H, (h + 1) * H)
                        dve.wait_ge(down, 2 * t + h + 3)
                        nc.vector.tensor_tensor(x2[:, par, at], ps_v[h][:, :], x2[:, par, at], ALU.add).then_inc(out_ready, 1)

                conv_input(0, 0, 1)
                y_split_lo(0)
                conv_input(1, 1, 1)
                residual(0, 0, 1, 0)
                residual(0, 0, 1, 1)
                y_split_lo(1)
                norm_constants(0)

                def step_a(t):
                    x_split_lo(t - 1)

                def step_b(t):
                    route(t - 1)
                    hidden(t - 1)
                    gated(t - 1)
                    m_split_lo(t - 1)

                with dve.Fori(0, MAIN // 2) as it:
                    for i in range(2):
                        t, par = 2 * it + 1 + i, 1 - i
                        use = it + 1 + i
                        step_a(t)
                        residual(t, par, use, 0)
                        conv_input(t + 1, 1 - par, it + 2)
                        step_b(t)
                        residual(t, par, use, 1)
                        norm_constants(t)
                        y_split_lo(t + 1)
                        output(t - 1, 1 - par)
                for t in range(MAIN + 1, NT + 1):
                    par = t % 2
                    step_a(t)
                    if t < NT:
                        residual(t, par, t // 2 + 1, 0)
                    if t + 1 < NT:
                        conv_input(t + 1, 1 - par, (t + 1) // 2 + 1)
                    step_b(t)
                    if t < NT:
                        residual(t, par, t // 2 + 1, 1)
                        norm_constants(t)
                    if t + 1 < NT:
                        y_split_lo(t + 1)
                    output(t - 1, 1 - par)

            @block.tensor
            def _(pe):
                def y_transposes(t, par):
                    if not isinstance(t, int) or t >= 1:
                        pe.wait_ge(y_lo_ready, t)
                    if not isinstance(t, int) or t >= 2:
                        pe.wait_ge(x_lo_ready, t - 1)
                    pe.wait_ge(y_ready, t + 3)
                    for k in range(KD):
                        r = nc.tensor.transpose(ps_t[:, k, :], ht[:, par, k * P:(k + 1) * P], keep.ident[:, :])
                    r.then_inc(y_tr, 1)

                def x_transposes(t):
                    pe.wait_ge(y_lo_ready, t + 2 if not isinstance(t, int) else min(t + 2, NT))
                    pe.wait_ge(xn_ready, t + 1)
                    for k in range(KD):
                        r = nc.tensor.transpose(ps_t[:, k, :], xn[:, k * P:(k + 1) * P], keep.ident[:, :])
                    r.then_inc(x_tr, 1)

                def three(out, hi, lo, w_hi, w_lo, start, stop):
                    nc.tensor.matmul(out, hi, w_hi, start=start, stop=False)
                    nc.tensor.matmul(out, hi, w_lo, start=False, stop=False)
                    return nc.tensor.matmul(out, lo, w_hi, start=False, stop=stop)

                def conv2(t, h, k0, k1):
                    at = slice(h * H, (h + 1) * H)
                    if k0 == 0:
                        pe.wait_ge(y_lo_ready, t + 1)
                        pe.wait_ge(biased, 2 * t + h + 1)
                    for k in range(k0, k1):
                        r = three(ps_u[h][:, :], y_hi[:, k, :], y_lo[:, k, :], keep.w_hi[:, k, at], keep.w_lo[:, k, at],
                                  k == 0, k == KD - 1)
                    if k1 == KD:
                        r.then_inc(conv, 1)

                def router_and_up(t):
                    pe.wait_ge(x_lo_ready, t + 1)
                    if not isinstance(t, int) or t >= 1:
                        pe.wait_ge(m_lo_ready, t)
                    for k in range(KD):
                        nc.tensor.matmul(ps_r, x_hi[:, k, :], rw[:, k, :, :].rearrange("p v e -> p (v e)"),
                                         start=k == 0, stop=False)
                        r = nc.tensor.matmul(ps_r[:, 0:EX], x_lo[:, k, :], rw[:, k, 0, :], start=False, stop=k == KD - 1)
                    r.then_inc(routed, 1)
                    if not isinstance(t, int) or t >= 1:
                        pe.wait_ge(gate_ready, t)
                    for k in range(KD):
                        r = three(ps_f[:, :], x_hi[:, k, :], x_lo[:, k, :], keep.f1_hi[:, k, :], keep.f1_lo[:, k, :],
                                  k == 0, k == KD - 1)
                    r.then_inc(up, 1)

                def m_transposes(t):
                    pe.wait_ge(hid_ready, t + 1)
                    nc.tensor.transpose(ps_g, gate3[:, :, :].rearrange("p v e -> p (v e)").bitcast(F32), keep.ident[:, :])
                    for k in range(KF):
                        r = nc.tensor.transpose(ps_m[:, k, :], hid[:, k * P:(k + 1) * P], keep.ident[:, :])
                    r.then_inc(m_tr, 1)

                def down_half(t, h):
                    at = slice(h * H, (h + 1) * H)
                    if h == 0:
                        pe.wait_ge(gate_ready, t + 1)
                    pe.wait_ge(out_ready, 2 * t + h + 1)
                    nc.tensor.matmul(ps_v[h][:, :], gate_t[:, :], fb2[:, at], start=True, stop=False)
                    if h == 0:
                        pe.wait_ge(m_lo_ready, t + 1)
                    for k in range(KF):
                        r = three(ps_v[h][:, :], m_hi[:, k, :], m_lo[:, k, :], keep.f2_hi[:, k, at], keep.f2_lo[:, k, at],
                                  False, k == KF - 1)
                    r.then_inc(down, 1)

                pe.wait_ge(set_up, 5)
                y_transposes(0, 0)
                conv2(0, 0, 0, KD)
                conv2(0, 1, 0, KD)
                y_transposes(1, 1)
                with pe.Fori(0, MAIN // 2) as it:
                    for i in range(2):
                        t = 2 * it + 1 + i
                        x_transposes(t - 1)
                        conv2(t, 0, 0, KD)
                        router_and_up(t - 1)
                        conv2(t, 1, 0, KD - 2)
                        m_transposes(t - 1)
                        conv2(t, 1, KD - 2, KD)
                        down_half(t - 1, 0)
                        y_transposes(t + 1, i)
                        down_half(t - 1, 1)
                for t in range(MAIN + 1, NT + 1):
                    x_transposes(t - 1)
                    if t < NT:
                        conv2(t, 0, 0, KD)
                    router_and_up(t - 1)
                    if t < NT:
                        conv2(t, 1, 0, KD - 2)
                    m_transposes(t - 1)
                    if t < NT:
                        conv2(t, 1, KD - 2, KD)
                    down_half(t - 1, 0)
                    if t + 1 < NT:
                        y_transposes(t + 1, (t + 1) % 2)
                    down_half(t - 1, 1)


class Names:
    pass


def build(nc, x, src, dst, pe, w1, b1, gamma, beta, w2, b2, rwt, f1t, fb1, f2t, fb2, out):
    s = Shapes(x, src, f1t)
    io, keep = Names(), Names()
    io.x, io.src, io.dst, io.pe, io.b1, io.gamma, io.beta = x, src, dst, pe, b1, gamma, beta
    io.b2, io.rwt, io.fb1, io.fb2, io.out = b2, rwt, fb1.rearrange("e f -> (e f)"), fb2, out
    io.h1 = nc.dram_tensor("h1_rows", (s.N, s.D), F32, kind="Internal").ap()
    io.sums = nc.dram_tensor("slot_sums", (s.EPAD, s.D), F32, kind="Internal").ap()
    chunks = lambda w: w.rearrange("(k p) n -> k p n", p=P)

    with ExitStack() as every, ExitStack() as mk:
        def sb(stack, name, shape, dt=F32, side=None):
            return stack.enter_context(nc.sbuf_tensor(name, shape, dt, side=side))

        keep.ident = sb(every, "ident", [P, P])
        keep.one = sb(every, "one", [P, 1])
        keep.zero = sb(every, "zero", [P, 1])
        keep.iota_e = sb(every, "iota_e", [P, 8])
        keep.dinv2 = sb(every, "dinv2", [P, s.A])
        keep.has_dinv = sb(every, "has_dinv", [P, s.A])
        keep.node_idx = sb(every, "node_idx", [P, s.A], I32)
        with ExitStack() as edges:
            keep.ones = sb(edges, "ones", [P, P])
            keep.dinv = sb(edges, "dinv", [P, s.A])
            keep.dst_row = sb(edges, "dst_row", [P, s.EPAD], U16)
            keep.dst_col = sb(edges, "dst_col", [P, s.ET])
            keep.src_idx = sb(edges, "src_idx", [P, s.ET], I32)
            keep.prev_idx = sb(edges, "prev_idx", [P, s.ET], I32)
            keep.sum_idx = sb(edges, "sum_idx", [P, s.ET], I32)
            keep.has_prev = sb(edges, "has_prev", [P, s.ET])
            keep.dinv_src = sb(edges, "dinv_src", [P, s.ET])
            keep.b1 = sb(edges, "b1", [P, s.D])
            keep.acc = sb(edges, "acc", [P, s.D])
            keep.acc2 = sb(edges, "acc2", [P, s.D])
            edge_tables(nc, s, io, keep, mk)
            keep.w_hi = sb(every, "w_hi", [P, s.KD, s.D], F32R, side="right")
            keep.w_lo = sb(every, "w_lo", [P, s.KD, s.D], F32R, side="right")
            conv_w = lambda w: [(chunks(w)[k], keep.w_hi[:, k, :], keep.w_lo[:, k, :]) for k in range(s.KD)]
            message_sums(nc, s, 1, io, keep, mk, conv_w(w1), [(b1, keep.b1)])
            conv1(nc, s, io, keep, mk)
            keep.f1_hi = sb(every, "f1_hi", [P, s.KD, s.F], F32R, side="right")
            keep.f1_lo = sb(every, "f1_lo", [P, s.KD, s.F], F32R, side="right")
            keep.f2_hi = sb(every, "f2_hi", [P, s.KF, s.D], F32R, side="right")
            keep.f2_lo = sb(every, "f2_lo", [P, s.KF, s.D], F32R, side="right")
            keep.bn_a = sb(every, "bn_a", [P, s.D], side="right")
            keep.bn_b = sb(every, "bn_b", [P, s.D], side="right")
            two = lambda w, k: w[:, 2 * k:2 * k + 2, :]
            up = [(f1t.rearrange("(k c p) n -> k p c n", c=2, p=P)[k], two(keep.f1_hi, k), two(keep.f1_lo, k))
                  for k in range(s.KD // 2)]
            down = [(chunks(f2t)[k], keep.f2_hi[:, k, :], keep.f2_lo[:, k, :]) for k in range(s.KF)]
            message_sums(nc, s, 2, io, keep, mk, conv_w(w2) + up + down, [(gamma, keep.bn_a), (beta, keep.bn_b)])
        keep.b2 = sb(every, "b2", [P, s.D])
        keep.fb1 = sb(every, "fb1", [P, s.F])
        conv2_ffn(nc, s, io, keep, mk)


def positions(n, d):
    import numpy as np
    pos = np.arange(n, dtype=np.float32)[:, None]
    div = np.exp(np.arange(0, d, 2, dtype=np.float32) * np.float32(-np.log(10000.0) / d))
    angle = pos * div
    return np.stack([np.sin(angle), np.cos(angle)], axis=-1).reshape(n, d).astype(np.float32)


def kernel(x, src, dst, L0_gnn_W1, L0_gnn_b1, L0_gnn_gamma, L0_gnn_beta, L0_gnn_W2, L0_gnn_b2,
           L0_ffn_router_w, L0_ffn_w1, L0_ffn_b1, L0_ffn_w2, L0_ffn_b2):
    import numpy as np
    import concourse.bacc as bacc
    from concourse.bass_utils import run_bass_kernel_spmd as run

    x = np.asarray(x)
    n, d = x.shape
    experts, hidden, _ = L0_ffn_w1.shape
    laid = {
        "x": x, "src": src, "dst": dst, "pe": positions(n, d),
        "w1": L0_gnn_W1, "b1": L0_gnn_b1, "gamma": L0_gnn_gamma, "beta": L0_gnn_beta, "w2": L0_gnn_W2, "b2": L0_gnn_b2,
        "router": np.asarray(L0_ffn_router_w).T,
        "f1": np.asarray(L0_ffn_w1).reshape(experts * hidden, d).T,
        "fb1": L0_ffn_b1,
        "f2": np.asarray(L0_ffn_w2).transpose(0, 2, 1).reshape(experts * hidden, d),
        "fb2": L0_ffn_b2,
    }
    nc = bacc.Bacc("TRN2", target_bir_lowering=False, num_devices=1)
    arrays, args = {}, []
    for name, a in laid.items():
        a = np.ascontiguousarray(a)
        arrays["in_" + name] = a
        args.append(nc.dram_tensor("in_" + name, a.shape, mybir.dt.from_np(a.dtype), kind="ExternalInput").ap())
    args.append(nc.dram_tensor("out_0", (n, d), F32, kind="ExternalOutput").ap())
    build(nc, *args)
    r = run(nc, [arrays], core_ids=[0])
    return r.results[0]["out_0"]
```

```python
import concourse.bass as bass
from concourse import mybir
from contextlib import ExitStack

F32 = mybir.dt.float32
F32R = mybir.dt.float32r
BF16 = mybir.dt.bfloat16
I32 = mybir.dt.int32
U32 = mybir.dt.uint32
U16 = mybir.dt.uint16
ACT = mybir.ActivationFunctionType
ALU = mybir.AluOpType

P = 128
EPS = 1e-5


class Shapes:

    def __init__(self, x, src, w1t):
        self.N, self.D = x.shape
        self.E = src.shape[0]
        self.KD = self.D // P
        self.H = self.D // 2
        self.R = self.D + 8
        self.NT = -(-self.N // P)
        self.LAST = self.N - (self.NT - 1) * P
        self.A = -(-self.NT // 16) * 16
        self.EP = -(-self.E // (4 * P)) * 2
        self.ET = 2 * self.EP
        self.EPAD = self.ET * P
        self.F = w1t.shape[1]
        self.KF = self.F // P
        self.PAD_DST = P * P - 1


def repeat(row):
    return row.rearrange("(k n) -> k n", k=1).to_broadcast([P, row.shape[0]])


def edge_tables(nc, s, io, keep, mk, pieces):
    ctx = ExitStack()
    with ctx:
        def sb(name, shape, dt=F32):
            return ctx.enter_context(nc.sbuf_tensor("tb_" + name, shape, dt))

        def sem(name):
            return mk.enter_context(nc.semaphore("tb_" + name))

        ET, A = s.ET, s.A
        full = s.E // P
        rest = s.E - full * P
        rows_i = sb("rows_i", [ET, 2, P], I32)
        rows_w = sb("rows_w", [ET, 2, P], I32)
        rows_f = sb("rows_f", [ET, 4, P])
        dst_all = sb("dst_all", [P, s.EPAD], I32)
        cols = sb("cols", [P, 4, ET])
        hot_low = sb("hot_low", [P, ET, P], BF16)
        hot_high = sb("hot_high", [P, ET, A], BF16)
        iota_a = sb("iota_a", [P, 1, A])
        iota_b = sb("iota_b", [P, 1, P])
        earlier = sb("earlier", [P, 2, 2 * P])
        counts = sb("counts", [P, 2, A])
        roots = sb("roots", [P, 2, A])
        count = sb("count", [P, ET])
        other = sb("other", [P, ET])
        away = sb("away", [P, ET])
        spare = sb("spare", [P, 2, ET])
        junk = sb("junk", [P, 2 * P])
        stage = sb("stage", [P, 2, s.D])
        ps_hist = ctx.enter_context(nc.psum_tensor("tb_hist", [P, A], F32))
        ps_cols = ctx.enter_context(nc.psum_tensor("tb_turned", [P, 4, ET], F32))

        consts = sem("consts")
        cleared = sem("cleared")
        rows_in = sem("rows_in")
        all_in = sem("all_in")
        w_in = [sem(f"w_in{i}") for i in range(2)]
        w_hi = sem("w_hi")
        w_lo = sem("w_lo")
        rows_ready = sem("rows_ready")
        cols_ps = sem("cols_ps")
        hot_ready = sem("hot_ready")
        hist_ready = sem("hist_ready")
        deg_ready = sem("deg_ready")
        std_ready = sem("std_ready")
        step = sem("step")

        with nc.Block() as block:
            @block.gpsimd
            def _(pool):
                pool.iota(iota_a[:, 0, :], pattern=[[1, A]], base=0, channel_multiplier=0,
                          allow_small_or_imprecise_dtypes=True)
                pool.iota(iota_b[:, 0, :], pattern=[[1, P]], base=0, channel_multiplier=0,
                          allow_small_or_imprecise_dtypes=True)
                pool.memset(keep.ident[:, :], 0.0).then_inc(consts, 1)
                pool.wait_ge(consts, 1)
                pool.affine_select(out=keep.ident[:, :], in_=keep.ident[:, :], compare_op=ALU.not_equal, fill=1.0,
                                   base=0, pattern=[[-1, P]], channel_multiplier=1).then_inc(consts, 1)
                pool.memset(keep.ones[:, :], 1.0)
                pool.memset(keep.one[:, :], 1.0)
                pool.memset(keep.zero[:, :], 0.0)
                pool.iota(keep.iota_e[:, :], pattern=[[1, 8]], base=0, channel_multiplier=0,
                          allow_small_or_imprecise_dtypes=True)
                pool.iota(spare[:, 0, :], pattern=[[0, ET]], base=s.N, channel_multiplier=1,
                          allow_small_or_imprecise_dtypes=True)
                pool.iota(spare[:, 1, :].rearrange("p (q i) -> p q i", i=2), pattern=[[0, ET // 2], [P, 2]], base=s.N,
                          channel_multiplier=1, allow_small_or_imprecise_dtypes=True)
                pool.memset(earlier[:, :, :], 1.0).then_inc(consts, 1)
                pool.wait_ge(consts, 3)
                for i in range(2):
                    r = pool.affine_select(out=earlier[:, i, :], in_=earlier[:, i, :], compare_op=ALU.is_gt, fill=0.0,
                                           base=i * P, pattern=[[-1, 2 * P]], channel_multiplier=1)
                r.then_inc(consts, 1)

            @block.sync
            def _(sp):
                sp.wait_ge(cleared, 1)
                for n, v in enumerate((io.src, io.dst)):
                    sp.dma_start(rows_i[0:full, n, :], v[0:full * P].rearrange("(k p) -> k p", p=P)).then_inc(rows_in, 16)
                    sp.dma_start(rows_i[full:full + 1, n, 0:rest],
                                 v[full * P:s.E].rearrange("(k p) -> k p", k=1)).then_inc(rows_in, 16)
                sp.wait_ge(cleared, 2)
                sp.dma_start(dst_all[:, 0:s.E], repeat(io.dst)).then_inc(all_in, 16)
                for n, (w, _hi, _lo) in enumerate(pieces):
                    if n >= 2:
                        sp.wait_ge(w_lo, n - 1)
                    sp.dma_start(stage[:, n % 2, :], w).then_inc(w_in[n % 2], 16)

            @block.vector
            def _(dve):
                done = [0]

                def then(ins):
                    done[0] += 1
                    ins.then_inc(step, 1)
                    dve.wait_ge(step, done[0])

                nc.vector.memset(rows_i[:, 0, :], 0)
                nc.vector.memset(rows_i[:, 1, :], s.PAD_DST).then_inc(cleared, 1)
                nc.vector.memset(dst_all[:, s.E:], s.PAD_DST).then_inc(cleared, 1)
                dve.wait_ge(rows_in, 64)
                nc.vector.tensor_single_scalar(rows_w[:, 0, :], rows_i[:, 1, :], P - 1, ALU.bitwise_and)
                then(nc.vector.tensor_single_scalar(rows_w[:, 1, :], rows_i[:, 1, :], 7, ALU.arith_shift_right))
                nc.vector.tensor_copy(rows_f[:, 0:2, :], rows_i[:, :, :])
                nc.vector.tensor_copy(rows_f[:, 2:4, :], rows_w[:, :, :]).then_inc(rows_ready, 1)
                dve.wait_ge(cols_ps, 1)
                then(nc.vector.tensor_copy(cols[:, :, :], ps_cols[:, :, :]))

                def one_hot(out, iota, col, n):
                    return nc.vector.tensor_tensor(out[:, :, :], iota[:, :, :].to_broadcast([P, ET, n]),
                                                   col.unsqueeze(2).to_broadcast([P, ET, n]), ALU.is_equal)

                dve.wait_ge(consts, 2)
                one_hot(hot_low, iota_b, cols[:, 2, :], P)
                one_hot(hot_high, iota_a, cols[:, 3, :], A).then_inc(hot_ready, 1)
                nc.vector.tensor_copy(keep.dst_col[:, :], cols[:, 1, :])
                nc.vector.tensor_copy(keep.src_idx[:, :], cols[:, 0, :])
                dve.wait_ge(all_in, 16)
                then(nc.vector.tensor_copy(keep.dst_row[:, :], dst_all[:, :]))
                dve.wait_ge(hist_ready, 1)
                nc.vector.tensor_scalar_add(counts[:, 0, :], ps_hist[:, :], 1.0)
                nc.vector.tensor_single_scalar(counts[:, 1, :], ps_hist[:, :], 1.0, ALU.max).then_inc(deg_ready, 1)
                for n, (w, hi, lo) in enumerate(pieces):
                    dve.wait_ge(w_hi, n + 1)
                    nc.vector.tensor_tensor(lo, stage[:, n % 2, :], hi.bitcast(F32), ALU.subtract).then_inc(w_lo, 1)
                dve.wait_ge(std_ready, 1)
                weights = keep.weights[:, :].rearrange("p (a v) -> p a v", v=4)
                then(nc.vector.reciprocal(roots[:, :, :], roots[:, :, :]))
                nc.vector.tensor_copy(keep.dinv[:, :], roots[:, 0, :])
                nc.vector.tensor_copy(weights[:, :, 0], roots[:, 0, :])
                then(nc.vector.tensor_single_scalar(weights[:, :, 3], counts[:, 0, :], 1.5, ALU.is_lt))
                nc.vector.tensor_tensor(weights[:, :, 3], weights[:, :, 3], keep.dinv[:, :], ALU.mult)
                then(nc.vector.tensor_tensor(weights[:, :, 1], roots[:, 0, :], roots[:, 1, :], ALU.mult))
                nc.vector.tensor_tensor(weights[:, :, 2], weights[:, :, 1], roots[:, 1, :], ALU.mult)
                nc.vector.tensor_tensor(keep.dinv2[:, :], keep.dinv[:, :], keep.dinv[:, :], ALU.mult)
                dve.wait_ge(consts, 4)
                for k in range(ET):
                    q, i = k // 2, k % 2
                    then(nc.vector.scalar_tensor_tensor(
                        out=junk[:, :], in0=keep.dst_row[:, 2 * P * q:2 * P * (q + 1)], scalar=keep.dst_col[:, k:k + 1],
                        in1=earlier[:, i, :], op0=ALU.is_equal, op1=ALU.mult, accum_out=count[:, k:k + 1]))
                then(nc.vector.tensor_single_scalar(other[:, :], keep.dst_col[:, :], float(s.PAD_DST) - 0.5, ALU.is_gt))
                nc.vector.tensor_tensor(count[:, :], count[:, :], other[:, :], ALU.add)
                then(nc.vector.tensor_tensor(away[:, :], spare[:, 0, :], keep.dst_col[:, :], ALU.subtract))
                then(nc.vector.tensor_tensor(away[:, :], away[:, :], other[:, :], ALU.mult))
                nc.vector.tensor_tensor(keep.dst_idx[:, :], away[:, :], keep.dst_col[:, :], ALU.add)
                then(nc.vector.tensor_single_scalar(other[:, :], count[:, :], 0.5, ALU.is_gt))
                then(nc.vector.tensor_tensor(away[:, :], spare[:, 1, :], keep.dst_col[:, :], ALU.subtract))
                then(nc.vector.tensor_tensor(away[:, :], away[:, :], other[:, :], ALU.mult))
                nc.vector.tensor_tensor(keep.add_idx[:, :], away[:, :], keep.dst_col[:, :], ALU.add)

            @block.scalar
            def _(act):
                for n, (_w, hi, _lo) in enumerate(pieces):
                    act.wait_ge(w_in[n % 2], 16 * (n // 2 + 1))
                    nc.scalar.copy(hi, stage[:, n % 2, :]).then_inc(w_hi, 1)
                act.wait_ge(deg_ready, 1)
                nc.scalar.activation(roots[:, :, :], counts[:, :, :], ACT.Sqrt).then_inc(std_ready, 1)

            @block.tensor
            def _(pe):
                pe.wait_ge(consts, 2)
                pe.wait_ge(rows_ready, 1)
                for v in range(4):
                    r = nc.tensor.transpose(ps_cols[:, v, :], rows_f[:, v, :], keep.ident[0:ET, 0:ET])
                r.then_inc(cols_ps, 1)
                pe.wait_ge(hot_ready, 1)
                for k in range(ET):
                    r = nc.tensor.matmul(ps_hist[:, :], hot_low[:, k, :], hot_high[:, k, :], start=k == 0, stop=k == ET - 1)
                r.then_inc(hist_ready, 1)


def conv1(nc, s, io, keep, mk):
    ctx = ExitStack()
    with ctx:
        def sb(name, shape, dt=F32):
            return ctx.enter_context(nc.sbuf_tensor("c1_" + name, shape, dt))

        def sem(name):
            return mk.enter_context(nc.semaphore("c1_" + name))

        D, H, KD, NT, LAST, R = s.D, s.H, s.KD, s.NT, s.LAST, s.R
        xt = sb("xt", [P, 2, D])
        pt = sb("pt", [P, 2, D])
        y = sb("y", [P, 2, D])
        y_hi = sb("y_hi", [P, 2, KD, P], F32R)
        y_lo = sb("y_lo", [P, 2, KD, P], F32R)
        ut = sb("ut", [P, 2, R])
        sq = sb("sq", [P, D])
        zeros = sb("zeros", [P, R])
        stats = sb("stats", [P, 2, 2, 6])
        mv = sb("mv", [P, 2, 2])
        small = sb("small", [P, 2, 3])
        eps = sb("eps", [P, 1])
        ps_t = [ctx.enter_context(nc.psum_tensor(f"c1_t{i}", [P, KD, P], F32)) for i in range(2)]
        ps_u = [ctx.enter_context(nc.psum_tensor(f"c1_u{h}", [P, H], F32)) for h in range(2)]

        ready = sem("ready")
        x_in = [sem(f"x_in{i}") for i in range(2)]
        pe_in = [sem(f"pe_in{i}") for i in range(2)]
        dve_gate = sem("dve_gate")
        pool_gate = sem("pool_gate")
        ln_dve = sem("ln_dve")
        std_ready = sem("std_ready")
        normed = sem("normed")
        y_ready = sem("y_ready")
        transposed = sem("transposed")
        hi_ready = sem("hi_ready")
        lo_ready = sem("lo_ready")
        products = sem("products")
        u_ready = sem("u_ready")
        added = sem("added")
        squared = sem("squared")
        sq_added = sem("sq_added")
        u_out = [sem(f"u_out{i}") for i in range(2)]
        cleared = sem("cleared")

        rows = lambda t: P if not isinstance(t, int) or t < NT - 1 else LAST
        block_rows = lambda ap, t: ap[bass.ds(t * P, rows(t)), :]
        MAIN = NT - 3

        with nc.Block() as block:
            @block.sync
            def _(sp):
                def loads(t, par):
                    sp.wait_ge(normed, t + 1)
                    sp.dma_start(xt[0:rows(t), par, :], block_rows(io.x, t)).then_inc(x_in[par], 16)
                    sp.wait_ge(y_ready, t + 1)
                    sp.dma_start(pt[0:rows(t), par, :], block_rows(io.pe, t)).then_inc(pe_in[par], 16)

                def clear(t):
                    sp.dma_start(block_rows(io.sums, t), zeros[0:rows(t), 0:D]).then_inc(cleared, 16)

                sp.wait_ge(ready, 1)
                loads(0, 0)
                loads(1, 1)
                with sp.Fori(0, MAIN // 2) as it:
                    for par in range(2):
                        t = 2 * it + par
                        loads(t + 2, par)
                        clear(t)
                for t in range(MAIN, NT):
                    if t + 2 < NT:
                        loads(t + 2, t % 2)
                    clear(t)
                for i in range(2):
                    spare = slice(s.N + i * P, s.N + (i + 1) * P)
                    sp.dma_start(io.g[spare, :], zeros[:, :]).then_inc(cleared, 16)
                    sp.dma_start(io.sums[spare, :], zeros[:, 0:D]).then_inc(cleared, 16)
                sp.wait_ge(cleared, 16 * (NT + 4))
                for par in range(2):
                    sp.wait_ge(u_out[par], 32 * ((NT + 1 - par) // 2) + 32)

            @block.gpsimd
            def _(pool):
                for v, n in ((normed, 2), (y_ready, 2), (transposed, 2), (lo_ready, 2), (products, 4),
                             (u_ready, 2), (added, 2), (squared, 2), (sq_added, 1), (u_out[0], 32), (u_out[1], 32)):
                    pool.sem_inc(v, n)
                pool.memset(ut[:, :, D + 4:R], 0.0)
                pool.memset(zeros[:, :], 0.0)
                pool.memset(keep.acc[:, :], 0.0)
                pool.memset(keep.acc2[:, :], 0.0)
                pool.memset(eps[:, :], EPS).then_inc(ready, 1)
                pool.wait_ge(ready, 1)

                def add_squares(t, n):
                    pool.wait_ge(sq_added, t + 1)
                    pool.wait_ge(squared, t + 3)
                    pool.sem_inc(pool_gate, 1)
                    pool.tensor_tensor(keep.acc2[0:n, :], keep.acc2[0:n, :], sq[0:n, :], ALU.add).then_inc(sq_added, 1)

                with pool.Fori(0, MAIN) as t:
                    add_squares(t, P)
                for t in range(MAIN, NT):
                    add_squares(t, rows(t))

            @block.scalar
            def _(act):
                def norm(t, par):
                    act.wait_ge(ln_dve, 4 * t + 2)
                    nc.scalar.activation(small[:, par, 0:1], mv[:, par, 1:2], ACT.Sqrt, bias=eps[:, 0:1]).then_inc(std_ready, 1)
                    act.wait_ge(transposed, t + 1)
                    act.wait_ge(ln_dve, 4 * t + 4)
                    nc.scalar.activation(y[:, par, :], xt[:, par, :], ACT.Identity, scale=small[:, par, 1:2],
                                         bias=small[:, par, 2:3]).then_inc(normed, 1)

                def split_hi(t, par):
                    act.wait_ge(transposed, t + 3)
                    act.wait_ge(products, 2 * t + 2)
                    nc.scalar.copy(y_hi[:, par, :, :], ps_t[par][:, :, :]).then_inc(hi_ready, 1)

                def store_and_square(t, par):
                    act.wait_ge(u_ready, 2 * t + 4)
                    for to in (io.u, io.g):
                        act.dma_start(block_rows(to, t), ut[0:rows(t), par, :]).then_inc(u_out[par], 16)
                    act.wait_ge(sq_added, t + 1)
                    nc.scalar.activation(sq[:, :], ut[:, par, 0:D], ACT.Square,
                                         scale=ut[:, par, D + 3:D + 4]).then_inc(squared, 1)

                act.wait_ge(ready, 1)
                norm(0, 0)
                norm(1, 1)
                split_hi(0, 0)
                with act.Fori(0, MAIN // 2) as it:
                    for par in range(2):
                        t = 2 * it + par
                        split_hi(t + 1, 1 - par)
                        norm(t + 2, par)
                        store_and_square(t, par)
                for t in range(MAIN, NT):
                    if t + 1 < NT:
                        split_hi(t + 1, (t + 1) % 2)
                    if t + 2 < NT:
                        norm(t + 2, t % 2)
                    store_and_square(t, t % 2)

            @block.vector
            def _(dve):
                def norm_constants(t, par, use):
                    dve.wait_ge(x_in[par], 16 * use)
                    nc.vector.bn_stats(stats[:, par, 0, :], xt[:, par, 0:H])
                    nc.vector.bn_stats(stats[:, par, 1, :], xt[:, par, H:D]).then_inc(ln_dve, 1)
                    dve.wait_ge(ln_dve, 4 * t + 1)
                    dve.sem_inc(dve_gate, 1)
                    nc.vector.bn_aggr(mv[:, par, :], stats[:, par, :, :]).then_inc(ln_dve, 1)
                    dve.wait_ge(std_ready, t + 1)
                    nc.vector.reciprocal(small[:, par, 1:2], small[:, par, 0:1]).then_inc(ln_dve, 1)
                    dve.wait_ge(ln_dve, 4 * t + 3)
                    nc.vector.tensor_scalar(small[:, par, 2:3], mv[:, par, 0:1], small[:, par, 1:2], -1.0,
                                            ALU.mult, ALU.mult).then_inc(ln_dve, 1)

                def add_positions(t, par, use):
                    dve.wait_ge(pe_in[par], 16 * use)
                    dve.wait_ge(normed, t + 3)
                    nc.vector.tensor_tensor(y[:, par, :], y[:, par, :], pt[:, par, :], ALU.add).then_inc(y_ready, 1)

                def split_lo(t, par):
                    dve.wait_ge(hi_ready, t + 1)
                    nc.vector.tensor_tensor(y_lo[:, par, :, :], ps_t[par][:, :, :], y_hi[:, par, :, :].bitcast(F32),
                                            ALU.subtract).then_inc(lo_ready, 1)

                def evacuate(t, par, use):
                    dve.wait_ge(u_out[par], 32 * use + 32)
                    dve.wait_ge(squared, t + 1)
                    dve.wait_ge(added, t + 1)
                    nc.vector.tensor_tensor(ut[:, par, D:D + 4], keep.weights[:, bass.ds(4 * t, 4)],
                                            keep.one[:, 0:1].to_broadcast([P, 4]), ALU.mult)
                    for h in range(2):
                        dve.wait_ge(products, 2 * t + h + 5)
                        nc.vector.tensor_scalar(ut[:, par, h * H:(h + 1) * H], ps_u[h][:, :], keep.dinv[:, bass.ds(t, 1)],
                                                None, ALU.mult).then_inc(u_ready, 1)
                    n = rows(t)
                    dve.wait_ge(u_ready, 2 * t + 4)
                    dve.wait_ge(added, t + 2)
                    nc.vector.scalar_tensor_tensor(out=keep.acc[0:n, :], in0=ut[0:n, par, 0:D], scalar=ut[0:n, par, D + 3:D + 4],
                                                   in1=keep.acc[0:n, :], op0=ALU.mult, op1=ALU.add).then_inc(added, 1)

                dve.wait_ge(ready, 1)
                for t in range(2):
                    norm_constants(t, t, 1)
                    add_positions(t, t, 1)
                split_lo(0, 0)
                with dve.Fori(0, MAIN // 2) as it:
                    for par in range(2):
                        t = 2 * it + par
                        split_lo(t + 1, 1 - par)
                        norm_constants(t + 2, par, it + 2)
                        add_positions(t + 2, par, it + 2)
                        evacuate(t, par, it)
                for t in range(MAIN, NT):
                    if t + 1 < NT:
                        split_lo(t + 1, (t + 1) % 2)
                    if t + 2 < NT:
                        norm_constants(t + 2, t % 2, t // 2 + 2)
                        add_positions(t + 2, t % 2, t // 2 + 2)
                    evacuate(t, t % 2, t // 2)

            @block.tensor
            def _(pe):
                def transposes(t, par):
                    pe.wait_ge(lo_ready, t + 1)
                    pe.wait_ge(y_ready, t + 3)
                    for k in range(KD):
                        r = nc.tensor.transpose(ps_t[par][:, k, :], y[:, par, k * P:(k + 1) * P], keep.ident[:, :])
                    r.then_inc(transposed, 1)

                def multiply(t, par):
                    pe.wait_ge(lo_ready, t + 3)
                    for h in range(2):
                        pe.wait_ge(u_ready, 2 * t + h + 1)
                        at = slice(h * H, (h + 1) * H)
                        for k in range(KD):
                            hi, lo = y_hi[:, par, k, :], y_lo[:, par, k, :]
                            nc.tensor.matmul(ps_u[h][:, :], hi, keep.w_hi[:, k, at], start=k == 0, stop=False)
                            nc.tensor.matmul(ps_u[h][:, :], hi, keep.w_lo[:, k, at], start=False, stop=False)
                            r = nc.tensor.matmul(ps_u[h][:, :], lo, keep.w_hi[:, k, at], start=False, stop=k == KD - 1)
                        r.then_inc(products, 1)

                pe.wait_ge(ready, 1)
                transposes(0, 0)
                with pe.Fori(0, MAIN // 2) as it:
                    for par in range(2):
                        t = 2 * it + par
                        transposes(t + 1, 1 - par)
                        multiply(t, par)
                for t in range(MAIN, NT):
                    if t + 1 < NT:
                        transposes(t + 1, (t + 1) % 2)
                    multiply(t, t % 2)


def message_sums(nc, s, layer, io, keep, mk, weights, rows):
    ctx = ExitStack()
    tag = f"m{layer}_"
    with ctx:
        def sb(name, shape, dt=F32):
            return ctx.enter_context(nc.sbuf_tensor(tag + name, shape, dt))

        def sem(name):
            return mk.enter_context(nc.semaphore(tag + name))

        D, H, EP, R = s.D, s.H, s.EP, s.R
        W = R if layer == 1 else D
        target = io.g if layer == 1 else io.sums
        source = io.u if layer == 1 else io.g
        NB = 4
        z = sb("z", [P, NB, R])
        z_b = [z[:, b, 0:D] for b in range(NB)]
        if layer == 1:
            msg, sums = z_b, [sb(f"sums{b}", [P, R]) for b in range(NB)]
        else:
            msg = [sb(f"msg{b}", [P, D])[:, :] for b in range(NB)]
            sums = [sb(f"sums{b}", [P, D]) for b in range(2)] + [keep.acc, keep.acc2]
        same = sb("same", [P, 2, 2, 2 * P])
        g_idx = sb("g_idx", [P, NB], I32)
        a_idx = sb("a_idx", [P, NB], I32)
        eps = sb("eps", [P, 1])
        stage = sb("stage", [P, 2, D]) if layer == 1 else None
        sq = stage
        ps = [[ctx.enter_context(nc.psum_tensor(f"{tag}ps{j}{i}", [P, 2, H], F32)) for i in range(2)] for j in range(2)]

        ready = sem("ready")
        rows_in = sem("rows_in")
        col_sums = sem("col_sums")
        w_in = [sem(f"w_in{i}") for i in range(2)]
        w_hi = sem("w_hi")
        w_lo = sem("w_lo")
        z_in = [sem(f"z_in{b}") for b in range(NB)]
        idx_step = sem("idx_step")
        pool_gate = sem("pool_gate")
        times_a = sem("times_a")
        scaled = sem("scaled")
        msg_ready = sem("msg_ready")
        same_ready = sem("same_ready")
        summed = sem("summed")
        sums_ready = sem("sums_ready")
        sums_out = [sem(f"sums_out{b}") for b in range(NB)]
        squared = sem("squared")
        added = sem("added")
        bn_step = sem("bn_step")

        chunks = [w.shape[0] // P for w, _hi, _lo in weights]
        first_pair = [sum(chunks[:n]) for n in range(len(chunks) + 1)]
        assert first_pair[-1] <= EP

        offset = bass.IndirectOffsetOnAxis

        with nc.Block() as block:
            @block.sync
            def _(sp):
                for row, t in rows:
                    sp.dma_start(t[:, :], repeat(row)).then_inc(rows_in, 16)
                sp.wait_ge(ready, 1)
                for n, (w, _hi, _lo) in enumerate(weights):
                    with sp.Fori(0, chunks[n] // 2) as it:
                        for j in range(2):
                            k = 2 * it + j
                            sp.wait_ge(w_lo, k + (first_pair[n] + 1))
                            sp.dma_start(stage[:, j, 0:w.shape[1]], w[bass.ds(k * P, P), :]).then_inc(w_in[j], 16)
                if rows:
                    sp.wait_ge(rows_in, 16 * len(rows))

            @block.gpsimd
            def _(pool):
                for v, n in ((summed, 2), (sums_ready, 4), (added, 4), (msg_ready, 4), (w_lo, 2)):
                    pool.sem_inc(v, n)
                if layer == 1:
                    for b in range(NB):
                        pool.memset(sums[b][:, D:W], 0.0)
                pool.memset(eps[:, :], EPS).then_inc(ready, 1)
                pool.wait_ge(ready, 1)

                def gather_rows(k, b, pair, n):
                    if layer == 1:
                        pool.wait_ge(summed, pair + 1)
                    else:
                        pool.wait_ge(msg_ready, k + 1)
                    pool.sem_inc(pool_gate, 1)
                    pool.tensor_copy(g_idx[:, b:b + 1], keep.src_idx[:, bass.ds(k, 1)]).then_inc(idx_step, 1)
                    pool.wait_ge(idx_step, n + 1)
                    pool.sem_inc(pool_gate, 1)
                    pool.indirect_dma_start(z[:, b, :], None, source, offset(ap=g_idx[:, b:b + 1], axis=0),
                                            bounds_check=s.N - 1, oob_is_err=False).then_inc(z_in[b], 16)

                def add_to_target(q, par, use, n):
                    for i in range(2):
                        b = 2 * par + i
                        r = pool.tensor_copy(a_idx[:, b:b + 1], keep.add_idx[:, bass.ds(2 * q + i, 1)])
                    r.then_inc(idx_step, 1)
                    pool.wait_ge(idx_step, n + 1)
                    if not isinstance(q, int) or q >= 1:
                        for i in range(2):
                            pool.wait_ge(sums_out[2 * (1 - par) + i], 16 * (use + par))
                    for i in range(2):
                        b = 2 * par + i
                        pool.wait_ge(sums_ready, 2 * q + i + 5)
                        pool.sem_inc(pool_gate, 1)
                        pool.indirect_dma_start(target, offset(ap=a_idx[:, b:b + 1], axis=0), sums[b][:, :], None,
                                                compute_op=ALU.add).then_inc(sums_out[b], 16)

                def gather_pair(q, par, n):
                    for i in range(2):
                        gather_rows(2 * q + i, 2 * par + i, q, n + i)

                gather_pair(0, 0, 0)
                gather_pair(1, 1, 2)
                gather_pair(2, 0, 4)
                add_to_target(0, 0, 0, 6)
                with pool.Fori(0, EP // 2 - 2) as it:
                    for i in range(2):
                        q, par = 2 * it + 1 + i, 1 - i
                        gather_pair(q + 2, par, 3 * q + 4)
                        add_to_target(q, par, it + i, 3 * q + 6)
                gather_pair(EP - 1, 1, 3 * EP - 5)
                add_to_target(EP - 3, 1, EP // 2 - 2, 3 * EP - 3)
                add_to_target(EP - 2, 0, EP // 2 - 1, 3 * EP - 2)
                add_to_target(EP - 1, 1, EP // 2 - 1, 3 * EP - 1)
                for b in range(NB):
                    pool.wait_ge(sums_out[b], 16 * (EP // 2))
                if layer == 1:
                    pool.wait_ge(summed, EP + 2)
                    with pool.Fori(0, EP // 2) as it:
                        for b in range(NB):
                            k = NB * it + b
                            pool.wait_ge(added, k + 1)
                            pool.sem_inc(pool_gate, 1)
                            pool.tensor_copy(g_idx[:, b:b + 1], keep.dst_idx[:, bass.ds(k, 1)]).then_inc(idx_step, 1)
                            pool.wait_ge(idx_step, k + (3 * EP + 1))
                            pool.sem_inc(pool_gate, 1)
                            pool.indirect_dma_start(z[:, b, :], None, target,
                                                    offset(ap=g_idx[:, b:b + 1], axis=0)).then_inc(z_in[b], 16)

            @block.scalar
            def _(act):
                act.wait_ge(ready, 1)
                if layer == 2:
                    act.wait_ge(bn_step, 4)
                    nc.scalar.activation(msg[2], msg[2], ACT.Sqrt, bias=eps[:, 0:1]).then_inc(bn_step, 1)

                def relu(k, b):
                    act.wait_ge(scaled, k + 1)
                    nc.scalar.activation(msg[b], msg[b], ACT.Relu, scale=z[:, b, D:D + 1]).then_inc(msg_ready, 1)

                def evacuate(q, par, use):
                    act.wait_ge(summed, q + 3)
                    for i in range(2):
                        b = 2 * par + i
                        if not isinstance(q, int) or q >= 2:
                            act.wait_ge(sums_out[b], 16 * use)
                        nc.scalar.copy(sums[b][:, 0:D], ps[par][i][:, :, :].rearrange("p a n -> p (a n)")).then_inc(sums_ready, 1)

                def pair(q, par):
                    if layer == 2:
                        for i in range(2):
                            relu(2 * q + i, 2 * par + i)

                pair(0, 0)
                pair(1, 1)
                evacuate(0, 0, 0)
                pair(2, 0)
                evacuate(1, 1, 0)
                with act.Fori(0, EP // 2 - 2) as it:
                    pair(2 * it + 3, 1)
                    evacuate(2 * it + 2, 0, it + 1)
                    pair(2 * it + 4, 0)
                    evacuate(2 * it + 3, 1, it + 1)
                pair(EP - 1, 1)
                evacuate(EP - 2, 0, EP // 2 - 1)
                evacuate(EP - 1, 1, EP // 2 - 1)
                if layer == 1:
                    act.wait_ge(w_lo, first_pair[-1] + 2)
                    with act.Fori(0, EP // 2) as it:
                        for b in range(NB):
                            k = NB * it + b
                            act.wait_ge(z_in[b], 16 * it + (8 * EP + 16))
                            act.wait_ge(added, k + 3)
                            nc.scalar.activation(sq[:, b % 2, :], z[:, b, 0:D], ACT.Square,
                                                 scale=z[:, b, D + 1:D + 2]).then_inc(squared, 1)

            @block.vector
            def _(dve):
                dve.wait_ge(ready, 1)
                if layer == 2:
                    mean, t, var = msg[0], msg[1], msg[2]
                    dve.wait_ge(col_sums, 1)
                    for j in range(2):
                        at = slice(j * H, (j + 1) * H)
                        nc.vector.tensor_single_scalar(mean[:, at], ps[0][0][:, j, :], 1.0 / s.N, ALU.mult)
                        r = nc.vector.tensor_single_scalar(var[:, at], ps[0][1][:, j, :], 1.0 / s.N, ALU.mult)
                    r.then_inc(bn_step, 1)
                    dve.wait_ge(bn_step, 1)
                    nc.vector.tensor_tensor(t, mean, mean, ALU.mult).then_inc(bn_step, 1)
                    dve.wait_ge(bn_step, 2)
                    nc.vector.tensor_tensor(var, var, t, ALU.subtract).then_inc(bn_step, 1)
                    dve.wait_ge(bn_step, 3)
                    nc.vector.tensor_single_scalar(var, var, 0.0, ALU.max).then_inc(bn_step, 1)
                    dve.wait_ge(bn_step, 5)
                    nc.vector.reciprocal(t, var)
                    nc.vector.tensor_tensor(mean, mean, keep.b1[:, :], ALU.add).then_inc(bn_step, 1)
                    dve.wait_ge(bn_step, 6)
                    nc.vector.tensor_tensor(keep.bn_a[:, :], keep.bn_a[:, :], t, ALU.mult).then_inc(bn_step, 1)
                    dve.wait_ge(bn_step, 7)
                    nc.vector.tensor_tensor(t, keep.bn_a[:, :], mean, ALU.mult)
                    nc.vector.tensor_tensor(keep.b1[:, :], keep.bn_a[:, :], keep.b1[:, :], ALU.mult).then_inc(bn_step, 1)
                    dve.wait_ge(bn_step, 8)
                    nc.vector.tensor_tensor(keep.bn_b[:, :], keep.bn_b[:, :], t, ALU.subtract).then_inc(bn_step, 1)
                    dve.wait_ge(bn_step, 9)
                    nc.vector.tensor_tensor(keep.bn_b[:, :], keep.bn_b[:, :], keep.b1[:, :], ALU.add).then_inc(bn_step, 2)
                    dve.wait_ge(bn_step, 11)

                def message(k, b, use):
                    dve.wait_ge(z_in[b], 16 * use)
                    nc.vector.tensor_tensor(msg[b], z[:, b, 0:D], keep.bn_a[:, :], ALU.mult).then_inc(times_a, 1)
                    dve.wait_ge(times_a, k + 1)
                    nc.vector.scalar_tensor_tensor(out=msg[b], in0=msg[b], scalar=z[:, b, D:D + 1],
                                                   in1=keep.bn_b[:, :], op0=ALU.mult, op1=ALU.add).then_inc(scaled, 1)

                def equality(q, par):
                    dve.wait_ge(summed, q + 1)
                    for i in range(2):
                        r = nc.vector.tensor_scalar(same[:, par, i, :], keep.dst_row[:, bass.ds(2 * P * q, 2 * P)],
                                                    keep.dst_col[:, bass.ds(2 * q + i, 1)], None, ALU.is_equal)
                    r.then_inc(same_ready, 1)

                def pair(q, par, use):
                    equality(q, par)
                    if layer == 2:
                        for i in range(2):
                            message(2 * q + i, 2 * par + i, use)

                def split(n, k, use):
                    w, hi, lo = weights[n]
                    j, rows_w = use[0], stage[:, use[0], 0:w.shape[1]]
                    dve.wait_ge(w_in[j], 16 * use[1])
                    nc.vector.tensor_scalar(hi[:, bass.ds(k, 1), :].rearrange("p k n -> p (k n)"), rows_w, 1.0, None,
                                            ALU.mult).then_inc(w_hi, 1)
                    dve.wait_ge(w_hi, k + (first_pair[n] + 1))
                    nc.vector.tensor_tensor(lo[:, bass.ds(k, 1), :].rearrange("p k n -> p (k n)"), rows_w,
                                            hi[:, bass.ds(k, 1), :].rearrange("p k n -> p (k n)").bitcast(F32),
                                            ALU.subtract).then_inc(w_lo, 1)

                for n in range(len(weights)):
                    with dve.Fori(0, chunks[n] // 2) as it:
                        for j in range(2):
                            pair(2 * it + (first_pair[n] + j), j, it + (first_pair[n] // 2 + 1))
                            split(n, 2 * it + j, (j, it + (first_pair[n] // 2 + 1)))
                if first_pair[-1] < EP:
                    with dve.Fori(0, (EP - first_pair[-1]) // 2) as it:
                        for j in range(2):
                            pair(2 * it + (first_pair[-1] + j), j, it + (first_pair[-1] // 2 + 1))
                if layer == 1:
                    with dve.Fori(0, EP // 2) as it:
                        for b in range(NB):
                            k = NB * it + b
                            dve.wait_ge(z_in[b], 16 * it + (8 * EP + 16))
                            dve.wait_ge(added, k + 4)
                            nc.vector.scalar_tensor_tensor(out=keep.acc[:, :], in0=z[:, b, 0:D], scalar=z[:, b, D + 2:D + 3],
                                                           in1=keep.acc[:, :], op0=ALU.mult, op1=ALU.add)
                            dve.wait_ge(squared, k + 1)
                            nc.vector.tensor_tensor(keep.acc2[:, :], keep.acc2[:, :], sq[:, b % 2, :], ALU.add).then_inc(added, 1)

            @block.tensor
            def _(pe):
                if layer == 2:
                    for t, n in ((keep.acc, 0), (keep.acc2, 1)):
                        for j in range(2):
                            r = nc.tensor.matmul(ps[0][n][:, j, :], keep.ones[:, :], t[:, j * H:(j + 1) * H],
                                                 start=True, stop=True)
                    r.then_inc(col_sums, 1)
                    pe.wait_ge(bn_step, 1)

                def pair(q, par, use):
                    pe.wait_ge(same_ready, q + 1)
                    if layer == 1:
                        for i in range(2):
                            pe.wait_ge(z_in[2 * par + i], 16 * use)
                    else:
                        pe.wait_ge(msg_ready, 2 * q + 6)
                    pe.wait_ge(sums_ready, 2 * q + 2)
                    for j in range(2):
                        for h in range(2):
                            for i in range(2):
                                r = nc.tensor.matmul(ps[par][j][:, h, :], same[:, par, i, j * P:(j + 1) * P],
                                                     msg[2 * par + i][:, h * H:(h + 1) * H], start=i == 0, stop=i == 1)
                    r.then_inc(summed, 1)

                with pe.Fori(0, EP // 2) as it:
                    for par in range(2):
                        pair(2 * it + par, par, it + 1)


def conv2_ffn(nc, s, io, keep, mk):
    ctx = ExitStack()
    with ctx:
        def sb(name, shape, dt=F32):
            return ctx.enter_context(nc.sbuf_tensor("c2_" + name, shape, dt))

        def sem(name):
            return mk.enter_context(nc.semaphore("c2_" + name))

        D, H, KD, KF, F, NT, LAST = s.D, s.H, s.KD, s.KF, s.F, s.NT, s.LAST
        EX = 8
        ht = sb("ht", [P, 2, D])
        xt = sb("xt", [P, 2, D])
        et = sb("et", [P, 2, D])
        y_hi = sb("y_hi", [P, KD, P], F32R)
        y_lo = sb("y_lo", [P, KD, P], F32R)
        x2 = sb("x2", [P, 2, D])
        xn = sb("xn", [P, D])
        x_hi = sb("x_hi", [P, KD, P], F32R)
        x_lo = sb("x_lo", [P, KD, P], F32R)
        hid = sb("hid", [P, F])
        m_hi = sb("m_hi", [P, KF, P], F32R)
        m_lo = sb("m_lo", [P, KF, P], F32R)
        rw_f = xn[:, 0:KD * EX].rearrange("p (k e) -> p k e", e=EX)
        rw = sb("rw", [P, KD, 2, EX], F32R)
        fb2_f = x2[0:3 * EX, 0, :]
        fb2 = sb("fb2", [3 * EX, D], F32R)
        gate_t = sb("gate_t", [3 * EX, P], F32R)
        stats = sb("stats", [P, 2, 6])
        mv = sb("mv", [P, 2])
        small = sb("small", [P, 4])
        half_p = sb("half_p", [P, 2])
        log_b = sb("log_b", [P, EX])
        logit = sb("logit", [P, EX])
        top = sb("top", [P, EX])
        top_i = sb("top_i", [P, EX], U32)
        top_f = sb("top_f", [P, 2])
        diff = sb("diff", [P, 1])
        th = sb("th", [P, 1])
        prob = sb("prob", [P, 2])
        pick = sb("pick", [P, 2, EX])
        gate = sb("gate", [P, 1, EX])
        gate3 = sb("gate3", [P, 3, EX], F32R)
        mid = sb("mid", [3 * EX, 3])
        ps_t = ctx.enter_context(nc.psum_tensor("c2_t", [P, KD, P], F32))
        ps_u = [ctx.enter_context(nc.psum_tensor(f"c2_u{h}", [P, H], F32)) for h in range(2)]
        ps_v = [ctx.enter_context(nc.psum_tensor(f"c2_v{h}", [P, H], F32)) for h in range(2)]
        ps_f = ctx.enter_context(nc.psum_tensor("c2_f", [P, F], F32))
        ps_m = ctx.enter_context(nc.psum_tensor("c2_m", [P, KF, P], F32))
        ps_r = ps_m[:, 0, 0:2 * EX]
        ps_g = ps_f[0:3 * EX, 0:P]

        ready = sem("ready")
        rows_in = sem("rows_in")
        rest_in = sem("rest_in")
        set_up = sem("set_up")
        h_in = [sem(f"h_in{i}") for i in range(2)]
        x_in = [sem(f"x_in{i}") for i in range(2)]
        e_in = [sem(f"e_in{i}") for i in range(2)]
        pool_gate = sem("pool_gate")
        dve_gate = sem("dve_gate")
        bn_dve = sem("bn_dve")
        y_ready = sem("y_ready")
        y_tr = sem("y_tr")
        y_hi_ready = sem("y_hi_ready")
        y_lo_ready = sem("y_lo_ready")
        conv = sem("conv")
        biased = sem("biased")
        res = sem("res")
        ln_dve = sem("ln_dve")
        pw = sem("pw")
        xn_ready = sem("xn_ready")
        x_tr = sem("x_tr")
        x_hi_ready = sem("x_hi_ready")
        x_lo_ready = sem("x_lo_ready")
        routed = sem("routed")
        up = sem("up")
        route_dve = sem("route_dve")
        th_ready = sem("th_ready")
        hid_bias = sem("hid_bias")
        hid_gelu = sem("hid_gelu")
        hid_ready = sem("hid_ready")
        m_tr = sem("m_tr")
        m_hi_ready = sem("m_hi_ready")
        m_lo_ready = sem("m_lo_ready")
        gate_ready = sem("gate_ready")
        down = sem("down")
        out_ready = sem("out_ready")
        out_sent = [sem(f"out_sent{i}") for i in range(2)]

        rows = lambda t: P if not isinstance(t, int) or t < NT - 1 else LAST
        block_rows = lambda ap, t: ap[bass.ds(t * P, rows(t)), :]
        MAIN = NT - 5

        with nc.Block() as block:
            @block.sync
            def _(sp):
                def loads(t, par):
                    sp.wait_ge(y_tr, t + 1)
                    sp.dma_start(ht[0:rows(t), par, :], block_rows(io.g, t)[:, 0:D]).then_inc(h_in[par], 16)
                    sp.wait_ge(y_ready, t + 1)
                    sp.dma_start(et[0:rows(t), par, :], block_rows(io.sums, t)).then_inc(e_in[par], 16)
                    sp.wait_ge(res, 2 * t + 2)
                    sp.dma_start(xt[0:rows(t), par, :], block_rows(io.x, t)).then_inc(x_in[par], 16)

                def store(t, par):
                    sp.wait_ge(out_ready, 2 * t + 4)
                    sp.dma_start(block_rows(io.out, t), x2[0:rows(t), par, :]).then_inc(out_sent[par], 16)

                sp.wait_ge(ready, 1)
                loads(0, 0)
                loads(1, 1)
                for row, t in ((io.b2, keep.b2), (io.fb1, keep.fb1)):
                    n = row.shape[0]
                    sp.dma_start(t[:, :], row.rearrange("(k n) -> k n", k=1).to_broadcast([P, n])).then_inc(rows_in, 16)
                sp.dma_start(rw_f, io.rwt.rearrange("(k p) e -> p k e", p=P)).then_inc(rest_in, 16)
                for i in range(3):
                    sp.dma_start(fb2_f[i * EX:(i + 1) * EX, :], io.fb2).then_inc(rest_in, 16)
                loads(2, 0)
                with sp.Fori(0, MAIN // 2) as it:
                    for i in range(2):
                        t = 2 * it + 1 + i
                        loads(t + 2, 1 - i)
                        store(t - 1, i)
                for t in range(MAIN + 1, NT + 1):
                    if t + 2 < NT:
                        loads(t + 2, t % 2)
                    store(t - 1, (t - 1) % 2)
                for par in range(2):
                    sp.wait_ge(out_sent[par], 16 * ((NT + 1 - par) // 2) + 16)

            @block.gpsimd
            def _(pool):
                for v, n in ((y_ready, 2), (y_tr, 2), (conv, 2), (biased, 2), (res, 4), (x_tr, 1), (up, 1), (m_tr, 1),
                             (down, 2), (out_ready, 2), (out_sent[0], 16), (out_sent[1], 16)):
                    pool.sem_inc(v, n)
                pool.memset(half_p[:, 0:1], -0.5)
                pool.memset(half_p[:, 1:2], EPS)
                pool.iota(mid[:, 0:1], pattern=[[0, 1]], base=0, channel_multiplier=1,
                          allow_small_or_imprecise_dtypes=True).then_inc(ready, 1)
                pool.wait_ge(ready, 1)

                def root(t):
                    pool.wait_ge(ln_dve, 4 * t + 2)
                    pool.sem_inc(pool_gate, 1)
                    pool.tensor_tensor(small[:, 0:1], mv[:, 1:2], half_p[:, 1:2], ALU.add).then_inc(pw, 1)
                    pool.wait_ge(pw, 2 * t + 1)
                    pool.sem_inc(pool_gate, 1)
                    pool.tensor_tensor(small[:, 1:2], small[:, 0:1], half_p[:, 0:1], ALU.pow).then_inc(pw, 1)

                with pool.Fori(0, NT) as t:
                    root(t)

            @block.scalar
            def _(act):
                def y_split_hi(t):
                    act.wait_ge(y_tr, t + 3)
                    act.wait_ge(conv, 2 * t + 2)
                    nc.scalar.copy(y_hi[:, :, :], ps_t[:, :, :]).then_inc(y_hi_ready, 1)

                def norm(t, par):
                    act.wait_ge(x_tr, t + 1)
                    act.wait_ge(ln_dve, 4 * t + 4)
                    nc.scalar.activation(xn[:, :], x2[:, par, :], ACT.Identity, scale=small[:, 2:3],
                                         bias=small[:, 3:4]).then_inc(xn_ready, 1)

                def x_split_hi(t):
                    act.wait_ge(x_tr, t + 2)
                    act.wait_ge(up, t + 1)
                    nc.scalar.copy(x_hi[:, :, :], ps_t[:, :, :]).then_inc(x_hi_ready, 1)

                def route_and_gelu(t):
                    act.wait_ge(route_dve, 8 * t + 4)
                    nc.scalar.activation(th[:, :], diff[:, :], ACT.Tanh, scale=0.5).then_inc(th_ready, 1)
                    act.wait_ge(hid_bias, t + 1)
                    nc.scalar.activation(hid[:, :], hid[:, :], ACT.Gelu).then_inc(hid_gelu, 1)

                def m_split_hi(t):
                    act.wait_ge(m_tr, t + 2)
                    act.wait_ge(down, 2 * t + 2)
                    nc.scalar.copy(gate_t[:, :], ps_g).then_inc(gate_ready, 1)
                    nc.scalar.copy(m_hi[:, :, :], ps_m[:, :, :]).then_inc(m_hi_ready, 1)

                act.wait_ge(set_up, 1)
                nc.scalar.activation(th[:, :], mv[:, 0:1], ACT.Gelu)
                y_split_hi(0)
                y_split_hi(1)
                norm(0, 0)

                def step(t, par):
                    x_split_hi(t - 1)
                    route_and_gelu(t - 1)
                    m_split_hi(t - 1)

                def after(t, par):
                    y_split_hi(t + 1)
                    norm(t, par)

                with act.Fori(0, MAIN // 2) as it:
                    for i in range(2):
                        t = 2 * it + 1 + i
                        step(t, 1 - i)
                        y_split_hi(t + 1)
                        norm(t, 1 - i)
                for t in range(MAIN + 1, NT + 1):
                    step(t, t % 2)
                    if t + 1 < NT:
                        y_split_hi(t + 1)
                    if t < NT:
                        norm(t, t % 2)

            @block.vector
            def _(dve):
                dve.wait_ge(ready, 1)
                nc.vector.memset(mv[:, :], 0.0).then_inc(set_up, 1)
                dve.wait_ge(rest_in, 64)
                nc.vector.tensor_copy(rw[:, :, 0, :], rw_f)
                nc.vector.tensor_single_scalar(mid[:, 1:2], mid[:, 0:1], float(EX) - 0.5, ALU.is_gt)
                nc.vector.tensor_single_scalar(mid[:, 2:3], mid[:, 0:1], float(2 * EX) - 0.5, ALU.is_lt)
                nc.vector.tensor_copy(fb2[:, :], fb2_f).then_inc(set_up, 1)
                dve.wait_ge(set_up, 2)
                nc.vector.tensor_tensor(rw[:, :, 1, :], rw_f, rw[:, :, 0, :].bitcast(F32), ALU.subtract)
                nc.vector.tensor_tensor(mid[:, 1:2], mid[:, 1:2], mid[:, 2:3], ALU.mult)
                nc.vector.tensor_tensor(fb2_f, fb2_f, fb2[:, :].bitcast(F32), ALU.subtract).then_inc(set_up, 1)
                dve.wait_ge(set_up, 3)
                nc.vector.tensor_scalar(mid[:, 2:3], mid[:, 1:2], -1.0, 1.0, ALU.mult, ALU.add)
                nc.vector.tensor_single_scalar(fb2_f, fb2_f, mid[:, 1:2], ALU.mult).then_inc(set_up, 1)
                dve.wait_ge(set_up, 4)
                nc.vector.scalar_tensor_tensor(out=fb2[:, :], in0=fb2[:, :].bitcast(F32), scalar=mid[:, 2:3], in1=fb2_f,
                                               op0=ALU.mult, op1=ALU.add).then_inc(set_up, 1)
                dve.wait_ge(rows_in, 32)

                def conv_input(t, par, use):
                    dinv = keep.dinv[:, bass.ds(t, 1)]
                    dve.wait_ge(h_in[par], 16 * use)
                    nc.vector.tensor_tensor(ht[:, par, :], ht[:, par, :], keep.bn_a[:, :], ALU.mult).then_inc(bn_dve, 1)
                    dve.wait_ge(bn_dve, 3 * t + 1)
                    nc.vector.scalar_tensor_tensor(out=ht[:, par, :], in0=ht[:, par, :], scalar=dinv, in1=keep.bn_b[:, :],
                                                   op0=ALU.mult, op1=ALU.add).then_inc(bn_dve, 1)
                    dve.wait_ge(bn_dve, 3 * t + 2)
                    nc.vector.tensor_scalar(ht[:, par, :], ht[:, par, :], 0.0, keep.dinv2[:, bass.ds(t, 1)],
                                            ALU.max, ALU.mult).then_inc(bn_dve, 1)
                    dve.wait_ge(e_in[par], 16 * use)
                    dve.wait_ge(bn_dve, 3 * t + 3)
                    nc.vector.scalar_tensor_tensor(out=ht[:, par, :], in0=et[:, par, :], scalar=dinv,
                                                   in1=ht[:, par, :], op0=ALU.mult, op1=ALU.add).then_inc(y_ready, 1)

                def y_split_lo(t):
                    dve.wait_ge(y_hi_ready, t + 1)
                    nc.vector.tensor_tensor(y_lo[:, :, :], ps_t[:, :, :], y_hi[:, :, :].bitcast(F32),
                                            ALU.subtract).then_inc(y_lo_ready, 1)

                def residual(t, par, use, h):
                    at = slice(h * H, (h + 1) * H)
                    if h == 0:
                        dve.wait_ge(out_sent[par], 16 * use)
                        dve.wait_ge(x_in[par], 16 * use)
                    dve.wait_ge(conv, 2 * t + h + 3)
                    nc.vector.tensor_tensor(x2[:, par, at], ps_u[h][:, :], keep.b2[:, at], ALU.add).then_inc(biased, 1)
                    dve.wait_ge(biased, 2 * t + h + 3)
                    nc.vector.scalar_tensor_tensor(out=x2[:, par, at], in0=x2[:, par, at], scalar=0.0, in1=xt[:, par, at],
                                                   op0=ALU.max, op1=ALU.add).then_inc(res, 1)
                    dve.wait_ge(res, 2 * t + h + 5)
                    r = nc.vector.bn_stats(stats[:, h, :], x2[:, par, at])
                    if h == 1:
                        r.then_inc(ln_dve, 1)

                def norm_constants(t):
                    dve.wait_ge(ln_dve, 4 * t + 1)
                    dve.sem_inc(dve_gate, 1)
                    nc.vector.bn_aggr(mv[:, :], stats[:, :, :]).then_inc(ln_dve, 1)
                    dve.wait_ge(pw, 2 * t + 2)
                    nc.vector.tensor_tensor(small[:, 2:3], small[:, 1:2], keep.one[:, 0:1], ALU.mult).then_inc(ln_dve, 1)
                    dve.wait_ge(ln_dve, 4 * t + 3)
                    nc.vector.tensor_scalar(small[:, 3:4], mv[:, 0:1], small[:, 2:3], -1.0,
                                            ALU.mult, ALU.mult).then_inc(ln_dve, 1)

                def x_split_lo(t):
                    dve.wait_ge(x_hi_ready, t + 1)
                    nc.vector.tensor_tensor(x_lo[:, :, :], ps_t[:, :, :], x_hi[:, :, :].bitcast(F32),
                                            ALU.subtract).then_inc(x_lo_ready, 1)

                def route(t):
                    base = 8 * t
                    dve.wait_ge(routed, t + 1)
                    nc.vector.tensor_copy(log_b[:, :], ps_r[:, EX:2 * EX]).then_inc(route_dve, 1)
                    dve.wait_ge(route_dve, base + 1)
                    nc.vector.tensor_tensor(logit[:, :], ps_r[:, 0:EX], log_b[:, :], ALU.add).then_inc(route_dve, 1)
                    dve.wait_ge(route_dve, base + 2)
                    dve.sem_inc(dve_gate, 1)
                    nc.vector.max(top[:, :], logit[:, :]).then_inc(route_dve, 1)
                    dve.wait_ge(route_dve, base + 3)
                    dve.sem_inc(dve_gate, 1)
                    nc.vector.max_index(top_i[:, :], top[:, :], logit[:, :])
                    nc.vector.tensor_tensor(diff[:, :], top[:, 0:1], top[:, 1:2], ALU.subtract).then_inc(route_dve, 1)
                    dve.wait_ge(route_dve, base + 4)
                    nc.vector.tensor_scalar(top_f[:, :], top_i[:, 0:2], 1.0, None, ALU.mult)
                    dve.wait_ge(th_ready, t + 1)
                    nc.vector.tensor_scalar(prob[:, 0:1], th[:, :], 0.5, 0.5, ALU.mult, ALU.add)
                    nc.vector.tensor_scalar(prob[:, 1:2], th[:, :], -0.5, 0.5, ALU.mult, ALU.add).then_inc(route_dve, 1)
                    dve.wait_ge(route_dve, base + 5)
                    for i in range(2):
                        r = nc.vector.tensor_scalar(pick[:, i, :], keep.iota_e[:, :], top_f[:, i:i + 1], prob[:, i:i + 1],
                                                    ALU.is_equal, ALU.mult)
                    r.then_inc(route_dve, 1)
                    dve.wait_ge(route_dve, base + 6)
                    nc.vector.tensor_tensor(gate[:, 0, :], pick[:, 0, :], pick[:, 1, :], ALU.add).then_inc(route_dve, 1)
                    dve.wait_ge(route_dve, base + 7)
                    dve.wait_ge(m_tr, t + 1)
                    nc.vector.tensor_tensor(gate3[:, 0:2, :], gate[:, :, :].to_broadcast([P, 2, EX]),
                                            keep.zero[:, 0:1].unsqueeze(2).to_broadcast([P, 2, EX]),
                                            ALU.add).then_inc(route_dve, 1)
                    dve.wait_ge(route_dve, base + 8)
                    nc.vector.tensor_tensor(gate3[:, 2, :], gate[:, 0, :], gate3[:, 0, :].bitcast(F32), ALU.subtract)

                def hidden(t):
                    dve.wait_ge(m_tr, t + 1)
                    dve.wait_ge(up, t + 2)
                    nc.vector.tensor_tensor(hid[:, :], ps_f[:, :], keep.fb1[:, :], ALU.add).then_inc(hid_bias, 1)

                def gated(t):
                    dve.wait_ge(hid_gelu, t + 1)
                    hid_e = hid[:, :].rearrange("p (e f) -> p e f", e=EX)
                    nc.vector.tensor_tensor(hid_e, hid_e, gate[:, 0, :].unsqueeze(2).to_broadcast([P, EX, F // EX]),
                                            ALU.mult).then_inc(hid_ready, 1)

                def m_split_lo(t):
                    dve.wait_ge(m_hi_ready, t + 1)
                    nc.vector.tensor_tensor(m_lo[:, :, :], ps_m[:, :, :], m_hi[:, :, :].bitcast(F32),
                                            ALU.subtract).then_inc(m_lo_ready, 1)

                def output(t, par):
                    dve.wait_ge(xn_ready, t + 1)
                    for h in range(2):
                        at = slice(h * H, (h + 1) * H)
                        dve.wait_ge(down, 2 * t + h + 3)
                        nc.vector.tensor_tensor(x2[:, par, at], ps_v[h][:, :], x2[:, par, at], ALU.add).then_inc(out_ready, 1)

                conv_input(0, 0, 1)
                y_split_lo(0)
                conv_input(1, 1, 1)
                residual(0, 0, 1, 0)
                residual(0, 0, 1, 1)
                y_split_lo(1)
                norm_constants(0)

                def step_a(t):
                    x_split_lo(t - 1)

                def step_b(t):
                    route(t - 1)
                    hidden(t - 1)
                    gated(t - 1)
                    m_split_lo(t - 1)

                with dve.Fori(0, MAIN // 2) as it:
                    for i in range(2):
                        t, par = 2 * it + 1 + i, 1 - i
                        use = it + 1 + i
                        step_a(t)
                        residual(t, par, use, 0)
                        conv_input(t + 1, 1 - par, it + 2)
                        step_b(t)
                        residual(t, par, use, 1)
                        norm_constants(t)
                        y_split_lo(t + 1)
                        output(t - 1, 1 - par)
                for t in range(MAIN + 1, NT + 1):
                    par = t % 2
                    step_a(t)
                    if t < NT:
                        residual(t, par, t // 2 + 1, 0)
                    if t + 1 < NT:
                        conv_input(t + 1, 1 - par, (t + 1) // 2 + 1)
                    step_b(t)
                    if t < NT:
                        residual(t, par, t // 2 + 1, 1)
                        norm_constants(t)
                    if t + 1 < NT:
                        y_split_lo(t + 1)
                    output(t - 1, 1 - par)

            @block.tensor
            def _(pe):
                def y_transposes(t, par):
                    if not isinstance(t, int) or t >= 1:
                        pe.wait_ge(y_lo_ready, t)
                    if not isinstance(t, int) or t >= 2:
                        pe.wait_ge(x_lo_ready, t - 1)
                    pe.wait_ge(y_ready, t + 3)
                    for k in range(KD):
                        r = nc.tensor.transpose(ps_t[:, k, :], ht[:, par, k * P:(k + 1) * P], keep.ident[:, :])
                    r.then_inc(y_tr, 1)

                def x_transposes(t):
                    pe.wait_ge(y_lo_ready, t + 2 if not isinstance(t, int) else min(t + 2, NT))
                    pe.wait_ge(xn_ready, t + 1)
                    for k in range(KD):
                        r = nc.tensor.transpose(ps_t[:, k, :], xn[:, k * P:(k + 1) * P], keep.ident[:, :])
                    r.then_inc(x_tr, 1)

                def three(out, hi, lo, w_hi, w_lo, start, stop):
                    nc.tensor.matmul(out, hi, w_hi, start=start, stop=False)
                    nc.tensor.matmul(out, hi, w_lo, start=False, stop=False)
                    return nc.tensor.matmul(out, lo, w_hi, start=False, stop=stop)

                def conv2(t, h, k0, k1):
                    at = slice(h * H, (h + 1) * H)
                    if k0 == 0:
                        pe.wait_ge(y_lo_ready, t + 1)
                        pe.wait_ge(biased, 2 * t + h + 1)
                    for k in range(k0, k1):
                        r = three(ps_u[h][:, :], y_hi[:, k, :], y_lo[:, k, :], keep.w_hi[:, k, at], keep.w_lo[:, k, at],
                                  k == 0, k == KD - 1)
                    if k1 == KD:
                        r.then_inc(conv, 1)

                def router_and_up(t):
                    pe.wait_ge(x_lo_ready, t + 1)
                    if not isinstance(t, int) or t >= 1:
                        pe.wait_ge(m_lo_ready, t)
                    for k in range(KD):
                        nc.tensor.matmul(ps_r, x_hi[:, k, :], rw[:, k, :, :].rearrange("p v e -> p (v e)"),
                                         start=k == 0, stop=False)
                        r = nc.tensor.matmul(ps_r[:, 0:EX], x_lo[:, k, :], rw[:, k, 0, :], start=False, stop=k == KD - 1)
                    r.then_inc(routed, 1)
                    if not isinstance(t, int) or t >= 1:
                        pe.wait_ge(gate_ready, t)
                    for k in range(KD):
                        r = three(ps_f[:, :], x_hi[:, k, :], x_lo[:, k, :], keep.f1_hi[:, k, :], keep.f1_lo[:, k, :],
                                  k == 0, k == KD - 1)
                    r.then_inc(up, 1)

                def m_transposes(t):
                    pe.wait_ge(hid_ready, t + 1)
                    nc.tensor.transpose(ps_g, gate3[:, :, :].rearrange("p v e -> p (v e)").bitcast(F32), keep.ident[:, :])
                    for k in range(KF):
                        r = nc.tensor.transpose(ps_m[:, k, :], hid[:, k * P:(k + 1) * P], keep.ident[:, :])
                    r.then_inc(m_tr, 1)

                def down_half(t, h):
                    at = slice(h * H, (h + 1) * H)
                    if h == 0:
                        pe.wait_ge(gate_ready, t + 1)
                    pe.wait_ge(out_ready, 2 * t + h + 1)
                    nc.tensor.matmul(ps_v[h][:, :], gate_t[:, :], fb2[:, at], start=True, stop=False)
                    if h == 0:
                        pe.wait_ge(m_lo_ready, t + 1)
                    for k in range(KF):
                        r = three(ps_v[h][:, :], m_hi[:, k, :], m_lo[:, k, :], keep.f2_hi[:, k, at], keep.f2_lo[:, k, at],
                                  False, k == KF - 1)
                    r.then_inc(down, 1)

                pe.wait_ge(set_up, 5)
                y_transposes(0, 0)
                conv2(0, 0, 0, KD)
                conv2(0, 1, 0, KD)
                y_transposes(1, 1)
                with pe.Fori(0, MAIN // 2) as it:
                    for i in range(2):
                        t = 2 * it + 1 + i
                        x_transposes(t - 1)
                        conv2(t, 0, 0, KD)
                        router_and_up(t - 1)
                        conv2(t, 1, 0, KD - 2)
                        m_transposes(t - 1)
                        conv2(t, 1, KD - 2, KD)
                        down_half(t - 1, 0)
                        y_transposes(t + 1, i)
                        down_half(t - 1, 1)
                for t in range(MAIN + 1, NT + 1):
                    x_transposes(t - 1)
                    if t < NT:
                        conv2(t, 0, 0, KD)
                    router_and_up(t - 1)
                    if t < NT:
                        conv2(t, 1, 0, KD - 2)
                    m_transposes(t - 1)
                    if t < NT:
                        conv2(t, 1, KD - 2, KD)
                    down_half(t - 1, 0)
                    if t + 1 < NT:
                        y_transposes(t + 1, (t + 1) % 2)
                    down_half(t - 1, 1)


class Names:
    pass


def build(nc, x, src, dst, pe, w1, b1, gamma, beta, w2, b2, rwt, f1t, fb1, f2t, fb2, out):
    s = Shapes(x, src, f1t)
    io, keep = Names(), Names()
    io.x, io.src, io.dst, io.pe, io.b1, io.gamma, io.beta = x, src, dst, pe, b1, gamma, beta
    io.b2, io.rwt, io.fb1, io.fb2, io.out = b2, rwt, fb1.rearrange("e f -> (e f)"), fb2, out
    io.u = nc.dram_tensor("u_rows", (s.N, s.R), F32, kind="Internal").ap()
    io.g = nc.dram_tensor("g_rows", (s.N + 2 * P, s.R), F32, kind="Internal").ap()
    io.sums = nc.dram_tensor("sums_rows", (s.N + 2 * P, s.D), F32, kind="Internal").ap()

    with ExitStack() as every, ExitStack() as mk:
        def sb(stack, name, shape, dt=F32, side=None):
            return stack.enter_context(nc.sbuf_tensor(name, shape, dt, side=side))

        keep.ident = sb(every, "ident", [P, P])
        keep.one = sb(every, "one", [P, 1])
        keep.zero = sb(every, "zero", [P, 1])
        keep.iota_e = sb(every, "iota_e", [P, 8])
        keep.dinv2 = sb(every, "dinv2", [P, s.A])
        keep.dinv = sb(every, "dinv", [P, s.A])
        with ExitStack() as edges:
            keep.ones = sb(edges, "ones", [P, P])
            keep.weights = sb(edges, "weights", [P, 4 * s.A])
            keep.dst_row = sb(edges, "dst_row", [P, s.EPAD], U16)
            keep.dst_col = sb(edges, "dst_col", [P, s.ET])
            keep.src_idx = sb(edges, "src_idx", [P, s.ET], I32)
            keep.dst_idx = sb(edges, "dst_idx", [P, s.ET], I32)
            keep.add_idx = sb(edges, "add_idx", [P, s.ET], I32)
            keep.b1 = sb(edges, "b1", [P, s.D])
            keep.acc = sb(edges, "acc", [P, s.D])
            keep.acc2 = sb(edges, "acc2", [P, s.D])
            keep.w_hi = sb(every, "w_hi", [P, s.KD, s.D], F32R, side="right")
            keep.w_lo = sb(every, "w_lo", [P, s.KD, s.D], F32R, side="right")
            edge_tables(nc, s, io, keep, mk,
                        [(w1[k * P:(k + 1) * P, :], keep.w_hi[:, k, :], keep.w_lo[:, k, :]) for k in range(s.KD)])
            conv1(nc, s, io, keep, mk)
            keep.f1_hi = sb(every, "f1_hi", [P, s.KD, s.F], F32R, side="right")
            keep.f1_lo = sb(every, "f1_lo", [P, s.KD, s.F], F32R, side="right")
            keep.f2_hi = sb(every, "f2_hi", [P, s.KF, s.D], F32R, side="right")
            keep.f2_lo = sb(every, "f2_lo", [P, s.KF, s.D], F32R, side="right")
            keep.bn_a = sb(every, "bn_a", [P, s.D], side="right")
            keep.bn_b = sb(every, "bn_b", [P, s.D], side="right")
            message_sums(nc, s, 1, io, keep, mk,
                         [(w2, keep.w_hi, keep.w_lo), (f1t, keep.f1_hi, keep.f1_lo), (f2t, keep.f2_hi, keep.f2_lo)],
                         [(gamma, keep.bn_a), (beta, keep.bn_b), (b1, keep.b1)])
            message_sums(nc, s, 2, io, keep, mk, [], [])
        keep.b2 = sb(every, "b2", [P, s.D])
        keep.fb1 = sb(every, "fb1", [P, s.F])
        conv2_ffn(nc, s, io, keep, mk)


def positions(n, d):
    import numpy as np
    pos = np.arange(n, dtype=np.float32)[:, None]
    div = np.exp(np.arange(0, d, 2, dtype=np.float32) * np.float32(-np.log(10000.0) / d))
    angle = pos * div
    return np.stack([np.sin(angle), np.cos(angle)], axis=-1).reshape(n, d).astype(np.float32)


def kernel(x, src, dst, L0_gnn_W1, L0_gnn_b1, L0_gnn_gamma, L0_gnn_beta, L0_gnn_W2, L0_gnn_b2,
           L0_ffn_router_w, L0_ffn_w1, L0_ffn_b1, L0_ffn_w2, L0_ffn_b2):
    import numpy as np
    import concourse.bacc as bacc
    from concourse.bass_utils import run_bass_kernel_spmd as run

    x = np.asarray(x)
    n, d = x.shape
    experts, hidden, _ = L0_ffn_w1.shape
    laid = {
        "x": x, "src": src, "dst": dst, "pe": positions(n, d),
        "w1": L0_gnn_W1, "b1": L0_gnn_b1, "gamma": L0_gnn_gamma, "beta": L0_gnn_beta, "w2": L0_gnn_W2, "b2": L0_gnn_b2,
        "router": np.asarray(L0_ffn_router_w).T,
        "f1": np.asarray(L0_ffn_w1).reshape(experts * hidden, d).T,
        "fb1": L0_ffn_b1,
        "f2": np.asarray(L0_ffn_w2).transpose(0, 2, 1).reshape(experts * hidden, d),
        "fb2": L0_ffn_b2,
    }
    nc = bacc.Bacc("TRN2", target_bir_lowering=False, num_devices=1)
    arrays, args = {}, []
    for name, a in laid.items():
        a = np.ascontiguousarray(a)
        arrays["in_" + name] = a
        args.append(nc.dram_tensor("in_" + name, a.shape, mybir.dt.from_np(a.dtype), kind="ExternalInput").ap())
    args.append(nc.dram_tensor("out_0", (n, d), F32, kind="ExternalOutput").ap())
    build(nc, *args)
    r = run(nc, [arrays], core_ids=[0])
    return r.results[0]["out_0"]
```
